# Optimizing a Trainium2 kernel written in Bass

```python
import numpy as np
import jax
import jax.numpy as jnp

def _softmax(x, axis=-1):
    return jax.nn.softmax(x, axis=axis)

def _gelu(x):
    return jax.nn.gelu(x, approximate=True)

def _silu(x):
    return jax.nn.silu(x)

def _sigmoid(x):
    return jax.nn.sigmoid(x)

def _layernorm(x, axis=-1, eps=1e-05):
    m = jnp.mean(x, axis=axis, keepdims=True)
    v = jnp.var(x, axis=axis, keepdims=True)
    return (x - m) / jnp.sqrt(v + eps)

def _scatter_add(tgt, idx, src, axis=0):
    return tgt.at[idx].add(src)

def _segment_sum(src, seg, n):
    return jax.ops.segment_sum(src, seg, n)
kernel_name = 'mk_pixart_seq_d2_seqx_r8_df3585'

def setup_inputs(seed: int=0):
    np.random.seed(seed)
    _w = jnp.asarray

    def _rec_inputs():
        import jax
        import jax.numpy as jnp
        _rk = jax.random.key(seed)
        x = -0.0002928 + 1 * jax.random.normal(jax.random.fold_in(_rk, 1), (16, 128, 128), jnp.float32)
        _lenS = 128 - jax.random.randint(jax.random.fold_in(_rk, 7), (16,), 0, max(1, 128 // 4) + 1, jnp.int32)
        _lenS2 = 120 - jax.random.randint(jax.random.fold_in(_rk, 8), (16,), 0, max(1, 120 // 4) + 1, jnp.int32)
        cond_1024 = 0.0061147 + 1.02565 * jax.random.normal(jax.random.fold_in(_rk, 11), (16, 128), jnp.float32)
        _ctx_1024P = jax.random.normal(jax.random.fold_in(_rk, 12), (16, 16, 128), jnp.float32)
        _ctx_1024c = jax.random.dirichlet(jax.random.fold_in(_rk, 512), 0.3 * jnp.ones((16,), jnp.float32), (16, 120))
        _ctx_1024t = jnp.einsum('bsk,bkd->bsd', _ctx_1024c, _ctx_1024P)
        _ctx_1024t = _ctx_1024t * jax.lax.rsqrt(jnp.mean(jnp.square(_ctx_1024t)) + 1e-12) * 0.953939
        ctx_1024 = -0.00265004 + 0.998804 * (_ctx_1024t + 0.3 * jax.random.normal(jax.random.fold_in(_rk, 612), (16, 120, 128), jnp.float32))
        return (x, cond_1024, ctx_1024)
    x, cond_1024, ctx_1024 = _rec_inputs()

    def _L0_xcond_setup():
        import jax, jax.numpy as jnp
        import numpy as np
        LN_EPS = 1e-06

        def _ln(x):
            mu = jnp.mean(x, axis=-1, keepdims=True)
            var = jnp.var(x, axis=-1, keepdims=True)
            return (x - mu) * jax.lax.rsqrt(var + LN_EPS)
        key = jax.random.key(seed)
        H, NH = (128, 16)
        B, N, S = (4, 128, 77)
        MLP = int(H * 4.0)
        ks = jax.random.split(key, 20)
        s = 1.0 / np.sqrt(H)
        return {'x': jax.random.normal(ks[0], (B, N, H), jnp.float32), 'c': jax.random.normal(ks[1], (B, H), jnp.float32), 'context': jax.random.normal(ks[2], (B, S, H), jnp.float32), 'W_mod': jax.random.normal(ks[3], (H, 6 * H), jnp.float32) * s, 'b_mod': jnp.zeros((6 * H,), jnp.float32), 'W_qkv': jax.random.normal(ks[4], (H, 3 * H), jnp.float32) * s, 'b_qkv': jnp.zeros((3 * H,), jnp.float32), 'W_proj': jax.random.normal(ks[5], (H, H), jnp.float32) * s, 'b_proj': jnp.zeros((H,), jnp.float32), 'W_qc': jax.random.normal(ks[6], (H, H), jnp.float32) * s, 'b_qc': jnp.zeros((H,), jnp.float32), 'W_kvc': jax.random.normal(ks[7], (H, 2 * H), jnp.float32) * s, 'b_kvc': jnp.zeros((2 * H,), jnp.float32), 'W_cproj': jax.random.normal(ks[8], (H, H), jnp.float32) * s, 'b_cproj': jnp.zeros((H,), jnp.float32), 'W_mlp1': jax.random.normal(ks[9], (H, MLP), jnp.float32) * s, 'b_mlp1': jnp.zeros((MLP,), jnp.float32), 'W_mlp2': jax.random.normal(ks[10], (MLP, H), jnp.float32) * (1.0 / np.sqrt(MLP)), 'b_mlp2': jnp.zeros((H,), jnp.float32)}
    _L0_xcond_all = _L0_xcond_setup()
    _L0_xcond_in = {k: v for k, v in _L0_xcond_all.items() if k in ('W_mod', 'b_mod', 'W_qkv', 'b_qkv', 'W_proj', 'b_proj', 'W_qc', 'b_qc', 'W_kvc', 'b_kvc', 'W_cproj', 'b_cproj', 'W_mlp1', 'b_mlp1', 'W_mlp2', 'b_mlp2')}
    del _L0_xcond_all

    def _L1_xcond_setup():
        import jax, jax.numpy as jnp
        import numpy as np
        import math
        D_MODEL = 128
        N_HEADS = 16
        HEAD_DIM = D_MODEL // N_HEADS
        D_FF = 512
        EPS = 1e-05
        ROPE_BASE = 10000.0

        def _rope(t):
            L, Dh = (t.shape[1], t.shape[-1])
            half = Dh // 2
            inv_freq = 1.0 / ROPE_BASE ** (jnp.arange(half, dtype=t.dtype) / half)
            ang = jnp.arange(L, dtype=t.dtype)[:, None] * inv_freq[None, :]
            cos = jnp.cos(ang)[None, :, None, :]
            sin = jnp.sin(ang)[None, :, None, :]
            t1, t2 = (t[..., :half], t[..., half:])
            return jnp.concatenate([t1 * cos - t2 * sin, t2 * cos + t1 * sin], axis=-1)

        def _adaln(x, emb, w, b):
            e = emb[:, 0, :]
            gb = e @ w.T + b
            gamma, beta = jnp.split(gb, 2, axis=-1)
            mu = x.mean(-1, keepdims=True)
            var = x.var(-1, keepdims=True)
            xn = (x - mu) * jax.lax.rsqrt(var + EPS)
            return xn * (1.0 + gamma[:, None, :]) + beta[:, None, :]

        def _attn(q, k, v):
            scale = 1.0 / math.sqrt(HEAD_DIM)
            scores = jnp.einsum('bqhd,bkhd->bhqk', q, k) * scale
            w = jax.nn.softmax(scores, axis=-1)
            out = jnp.einsum('bhqk,bkhd->bqhd', w, v)
            B, Lq = (out.shape[0], out.shape[1])
            return out.reshape(B, Lq, D_MODEL)
        key = jax.random.key(seed)
        ks = jax.random.split(key, 24)
        s = 0.02
        inp = {'x': jax.random.normal(ks[0], (2, 256, D_MODEL), jnp.float32), 'noise_emb': jax.random.normal(ks[1], (2, 1, D_MODEL), jnp.float32), 'context': jax.random.normal(ks[2], (2, 128, D_MODEL), jnp.float32), 'ln1_w': jax.random.normal(ks[3], (2 * D_MODEL, D_MODEL), jnp.float32) * s, 'ln1_b': jax.random.normal(ks[4], (2 * D_MODEL,), jnp.float32) * s, 'ln2_w': jax.random.normal(ks[5], (2 * D_MODEL, D_MODEL), jnp.float32) * s, 'ln2_b': jax.random.normal(ks[6], (2 * D_MODEL,), jnp.float32) * s, 'ln3_w': jax.random.normal(ks[7], (2 * D_MODEL, D_MODEL), jnp.float32) * s, 'ln3_b': jax.random.normal(ks[8], (2 * D_MODEL,), jnp.float32) * s, 'qkv_w': jax.random.normal(ks[9], (3 * D_MODEL, D_MODEL), jnp.float32) * s, 'sa_out_w': jax.random.normal(ks[10], (D_MODEL, D_MODEL), jnp.float32) * s, 'q_w': jax.random.normal(ks[11], (D_MODEL, D_MODEL), jnp.float32) * s, 'k_w': jax.random.normal(ks[12], (D_MODEL, D_MODEL), jnp.float32) * s, 'v_w': jax.random.normal(ks[13], (D_MODEL, D_MODEL), jnp.float32) * s, 'ca_out_w': jax.random.normal(ks[14], (D_MODEL, D_MODEL), jnp.float32) * s, 'ffn_w1': jax.random.normal(ks[15], (D_FF, D_MODEL), jnp.float32) * s, 'ffn_b1': jax.random.normal(ks[16], (D_FF,), jnp.float32) * s, 'ffn_w2': jax.random.normal(ks[17], (D_MODEL, D_FF), jnp.float32) * s, 'ffn_b2': jax.random.normal(ks[18], (D_MODEL,), jnp.float32) * s}
        return inp
    _L1_xcond_all = _L1_xcond_setup()
    _L1_xcond_in = {k: v for k, v in _L1_xcond_all.items() if k in ('ln1_w', 'ln1_b', 'ln2_w', 'ln2_b', 'ln3_w', 'ln3_b', 'qkv_w', 'sa_out_w', 'q_w', 'k_w', 'v_w', 'ca_out_w', 'ffn_w1', 'ffn_b1', 'ffn_w2', 'ffn_b2')}
    del _L1_xcond_all
    return {'x': x, 'cond_1024': cond_1024, 'ctx_1024': ctx_1024, 'L0_xcond_W_mod': _L0_xcond_in['W_mod'], 'L0_xcond_b_mod': _L0_xcond_in['b_mod'], 'L0_xcond_W_qkv': _L0_xcond_in['W_qkv'], 'L0_xcond_b_qkv': _L0_xcond_in['b_qkv'], 'L0_xcond_W_proj': _L0_xcond_in['W_proj'], 'L0_xcond_b_proj': _L0_xcond_in['b_proj'], 'L0_xcond_W_qc': _L0_xcond_in['W_qc'], 'L0_xcond_b_qc': _L0_xcond_in['b_qc'], 'L0_xcond_W_kvc': _L0_xcond_in['W_kvc'], 'L0_xcond_b_kvc': _L0_xcond_in['b_kvc'], 'L0_xcond_W_cproj': _L0_xcond_in['W_cproj'], 'L0_xcond_b_cproj': _L0_xcond_in['b_cproj'], 'L0_xcond_W_mlp1': _L0_xcond_in['W_mlp1'], 'L0_xcond_b_mlp1': _L0_xcond_in['b_mlp1'], 'L0_xcond_W_mlp2': _L0_xcond_in['W_mlp2'], 'L0_xcond_b_mlp2': _L0_xcond_in['b_mlp2'], 'L1_xcond_ln1_w': _L1_xcond_in['ln1_w'], 'L1_xcond_ln1_b': _L1_xcond_in['ln1_b'], 'L1_xcond_ln2_w': _L1_xcond_in['ln2_w'], 'L1_xcond_ln2_b': _L1_xcond_in['ln2_b'], 'L1_xcond_ln3_w': _L1_xcond_in['ln3_w'], 'L1_xcond_ln3_b': _L1_xcond_in['ln3_b'], 'L1_xcond_qkv_w': _L1_xcond_in['qkv_w'], 'L1_xcond_sa_out_w': _L1_xcond_in['sa_out_w'], 'L1_xcond_q_w': _L1_xcond_in['q_w'], 'L1_xcond_k_w': _L1_xcond_in['k_w'], 'L1_xcond_v_w': _L1_xcond_in['v_w'], 'L1_xcond_ca_out_w': _L1_xcond_in['ca_out_w'], 'L1_xcond_ffn_w1': _L1_xcond_in['ffn_w1'], 'L1_xcond_ffn_b1': _L1_xcond_in['ffn_b1'], 'L1_xcond_ffn_w2': _L1_xcond_in['ffn_w2'], 'L1_xcond_ffn_b2': _L1_xcond_in['ffn_b2']}

def reference(x, cond_1024, ctx_1024, L0_xcond_W_mod, L0_xcond_b_mod, L0_xcond_W_qkv, L0_xcond_b_qkv, L0_xcond_W_proj, L0_xcond_b_proj, L0_xcond_W_qc, L0_xcond_b_qc, L0_xcond_W_kvc, L0_xcond_b_kvc, L0_xcond_W_cproj, L0_xcond_b_cproj, L0_xcond_W_mlp1, L0_xcond_b_mlp1, L0_xcond_W_mlp2, L0_xcond_b_mlp2, L1_xcond_ln1_w, L1_xcond_ln1_b, L1_xcond_ln2_w, L1_xcond_ln2_b, L1_xcond_ln3_w, L1_xcond_ln3_b, L1_xcond_qkv_w, L1_xcond_sa_out_w, L1_xcond_q_w, L1_xcond_k_w, L1_xcond_v_w, L1_xcond_ca_out_w, L1_xcond_ffn_w1, L1_xcond_ffn_b1, L1_xcond_ffn_w2, L1_xcond_ffn_b2):
    import jax
    import jax.numpy as jnp

    def _L0_xcond_ref(x, c, context, W_mod, b_mod, W_qkv, b_qkv, W_proj, b_proj, W_qc, b_qc, W_kvc, b_kvc, W_cproj, b_cproj, W_mlp1, b_mlp1, W_mlp2, b_mlp2):
        import jax, jax.numpy as jnp
        import numpy as np
        LN_EPS = 1e-06

        def _ln(x):
            mu = jnp.mean(x, axis=-1, keepdims=True)
            var = jnp.var(x, axis=-1, keepdims=True)
            return (x - mu) * jax.lax.rsqrt(var + LN_EPS)
        B, N, H = x.shape
        NH = 16
        hd = H // NH
        scale = hd ** (-0.5)
        c_proj = jax.nn.silu(c) @ W_mod + b_mod
        shift_a, scale_a, gate_a, shift_m, scale_m, gate_m = jnp.split(c_proj, 6, axis=-1)

        def modulate(t, shift, sc):
            return t * (1 + sc[:, None]) + shift[:, None]
        x_norm = modulate(_ln(x), shift_a, scale_a)
        qkv = x_norm @ W_qkv + b_qkv
        q, k, v = jnp.split(qkv, 3, axis=-1)
        q = q.reshape(B, N, NH, hd).transpose(0, 2, 1, 3)
        k = k.reshape(B, N, NH, hd).transpose(0, 2, 1, 3)
        v = v.reshape(B, N, NH, hd).transpose(0, 2, 1, 3)
        attn_w = jax.nn.softmax(jnp.einsum('bhqd,bhkd->bhqk', q, k) * scale, axis=-1)
        attn_out = jnp.einsum('bhqk,bhkd->bhqd', attn_w, v)
        attn_out = attn_out.transpose(0, 2, 1, 3).reshape(B, N, H)
        attn_out = attn_out @ W_proj + b_proj
        x = x + gate_a[:, None] * attn_out
        S = context.shape[1]
        q_c = _ln(x) @ W_qc + b_qc
        kv_c = _ln(context) @ W_kvc + b_kvc
        k_c, v_c = jnp.split(kv_c, 2, axis=-1)
        q_c = q_c.reshape(B, N, NH, hd).transpose(0, 2, 1, 3)
        k_c = k_c.reshape(B, S, NH, hd).transpose(0, 2, 1, 3)
        v_c = v_c.reshape(B, S, NH, hd).transpose(0, 2, 1, 3)
        c_attn_w = jax.nn.softmax(jnp.einsum('bhqd,bhsd->bhqs', q_c, k_c) * scale, axis=-1)
        c_attn_out = jnp.einsum('bhqs,bhsd->bhqd', c_attn_w, v_c)
        c_attn_out = c_attn_out.transpose(0, 2, 1, 3).reshape(B, N, H)
        c_attn_out = c_attn_out @ W_cproj + b_cproj
        x = x + c_attn_out
        x_norm2 = modulate(_ln(x), shift_m, scale_m)
        h = jax.nn.gelu(x_norm2 @ W_mlp1 + b_mlp1)
        h = h @ W_mlp2 + b_mlp2
        x = x + gate_m[:, None] * h
        return x

    def _L1_xcond_ref(x, noise_emb, context, ln1_w, ln1_b, ln2_w, ln2_b, ln3_w, ln3_b, qkv_w, sa_out_w, q_w, k_w, v_w, ca_out_w, ffn_w1, ffn_b1, ffn_w2, ffn_b2):
        import jax, jax.numpy as jnp
        import numpy as np
        import math
        D_MODEL = 128
        N_HEADS = 16
        HEAD_DIM = D_MODEL // N_HEADS
        D_FF = 512
        EPS = 1e-05
        ROPE_BASE = 10000.0

        def _rope(t):
            L, Dh = (t.shape[1], t.shape[-1])
            half = Dh // 2
            inv_freq = 1.0 / ROPE_BASE ** (jnp.arange(half, dtype=t.dtype) / half)
            ang = jnp.arange(L, dtype=t.dtype)[:, None] * inv_freq[None, :]
            cos = jnp.cos(ang)[None, :, None, :]
            sin = jnp.sin(ang)[None, :, None, :]
            t1, t2 = (t[..., :half], t[..., half:])
            return jnp.concatenate([t1 * cos - t2 * sin, t2 * cos + t1 * sin], axis=-1)

        def _adaln(x, emb, w, b):
            e = emb[:, 0, :]
            gb = e @ w.T + b
            gamma, beta = jnp.split(gb, 2, axis=-1)
            mu = x.mean(-1, keepdims=True)
            var = x.var(-1, keepdims=True)
            xn = (x - mu) * jax.lax.rsqrt(var + EPS)
            return xn * (1.0 + gamma[:, None, :]) + beta[:, None, :]

        def _attn(q, k, v):
            scale = 1.0 / math.sqrt(HEAD_DIM)
            scores = jnp.einsum('bqhd,bkhd->bhqk', q, k) * scale
            w = jax.nn.softmax(scores, axis=-1)
            out = jnp.einsum('bhqk,bkhd->bqhd', w, v)
            B, Lq = (out.shape[0], out.shape[1])
            return out.reshape(B, Lq, D_MODEL)
        B, L, D = x.shape
        L_ctx = context.shape[1]
        res = x
        xn = _adaln(x, noise_emb, ln1_w, ln1_b)
        qkv = xn @ qkv_w.T
        q, k, v = jnp.split(qkv, 3, axis=-1)
        q = _rope(q.reshape(B, L, N_HEADS, HEAD_DIM))
        k = _rope(k.reshape(B, L, N_HEADS, HEAD_DIM))
        v = v.reshape(B, L, N_HEADS, HEAD_DIM)
        sa = _attn(q, k, v) @ sa_out_w.T
        x = res + sa
        res = x
        xn = _adaln(x, noise_emb, ln2_w, ln2_b)
        q = _rope((xn @ q_w.T).reshape(B, L, N_HEADS, HEAD_DIM))
        k = _rope((context @ k_w.T).reshape(B, L_ctx, N_HEADS, HEAD_DIM))
        v = (context @ v_w.T).reshape(B, L_ctx, N_HEADS, HEAD_DIM)
        ca = _attn(q, k, v) @ ca_out_w.T
        x = res + ca
        res = x
        xn = _adaln(x, noise_emb, ln3_w, ln3_b)
        h = jax.nn.gelu(xn @ ffn_w1.T + ffn_b1, approximate=False)
        x = res + (h @ ffn_w2.T + ffn_b2)
        return x
    x = _L0_xcond_ref(x, cond_1024, ctx_1024, L0_xcond_W_mod, L0_xcond_b_mod, L0_xcond_W_qkv, L0_xcond_b_qkv, L0_xcond_W_proj, L0_xcond_b_proj, L0_xcond_W_qc, L0_xcond_b_qc, L0_xcond_W_kvc, L0_xcond_b_kvc, L0_xcond_W_cproj, L0_xcond_b_cproj, L0_xcond_W_mlp1, L0_xcond_b_mlp1, L0_xcond_W_mlp2, L0_xcond_b_mlp2)
    x = _L1_xcond_ref(x, cond_1024[:, None, :], ctx_1024, L1_xcond_ln1_w, L1_xcond_ln1_b, L1_xcond_ln2_w, L1_xcond_ln2_b, L1_xcond_ln3_w, L1_xcond_ln3_b, L1_xcond_qkv_w, L1_xcond_sa_out_w, L1_xcond_q_w, L1_xcond_k_w, L1_xcond_v_w, L1_xcond_ca_out_w, L1_xcond_ffn_w1, L1_xcond_ffn_b1, L1_xcond_ffn_w2, L1_xcond_ffn_b2)
    return x

_drawn_inputs = setup_inputs


def setup_inputs(seed=0):
    import zlib

    import numpy as np

    out = dict(_drawn_inputs(seed))
    spreads = {'L0_xcond_b_mod': (0.0, 0.1),
     'L0_xcond_b_qkv': (0.0, 0.1),
     'L0_xcond_b_proj': (0.0, 0.1),
     'L0_xcond_b_qc': (0.0, 0.512),
     'L0_xcond_b_kvc': (0.0, 0.1),
     'L0_xcond_b_cproj': (0.0, 0.1),
     'L0_xcond_b_mlp1': (0.0, 0.1),
     'L0_xcond_b_mlp2': (0.0, 0.1)}
    factors = {'L1_xcond_ln1_w': 5.636,
     'L1_xcond_ln1_b': 63.797,
     'L1_xcond_ln2_w': 8.0,
     'L1_xcond_ln2_b': 8.0,
     'L1_xcond_ln3_w': 4.324,
     'L1_xcond_ln3_b': 50.444,
     'L1_xcond_q_w': 8.0,
     'L1_xcond_k_w': 8.0,
     'L1_xcond_v_w': 2.862,
     'L1_xcond_ca_out_w': 2.926,
     'L1_xcond_ffn_b1': 8.0,
     'L1_xcond_ffn_b2': 4.035}
    for name, (base, spread) in spreads.items():
        noise = np.random.default_rng([zlib.crc32(name.encode()), seed]).standard_normal(out[name].shape)
        drawn = base * np.exp(spread * noise) if base else spread * noise
        out[name] = jnp.asarray(drawn.astype(out[name].dtype))
    for name, factor in factors.items():
        out[name] = (out[name] * factor).astype(out[name].dtype)
    return out
```

```python
from contextlib import ExitStack

import numpy as np

import concourse.bass as bass
from concourse import mybir

ALU = mybir.AluOpType
ACT = mybir.ActivationFunctionType
AX_X = mybir.AxisListType.X
F32 = mybir.dt.float32
F32R = mybir.dt.float32r

P = 128
D = 128
B = 16
NS_CTX = 120
H = 16
HD = D // H
SCALE = HD ** -0.5
CB = 4
CT = CB * P
STREAMS = B // CB
HG = 4
NG = H // HG
GH = H // 2
FF = 4
VW = HD + 1

WCOLS = {}


def _pack_names():
    names = [("mod", 6 * D), ("ln", 6 * D), ("condT", B),
             ("q0", D), ("k0", D), ("v0", D), ("o0", D),
             ("q1", D), ("k1", D), ("v1", D), ("o1", D), ("w1_0", FF * D), ("w2_0", FF * D),
             ("q2", D), ("q2s", D), ("k2", D), ("k2s", D), ("v2", D), ("o2", D),
             ("q3", D), ("q3s", D), ("k3", D), ("k3s", D), ("v3", D), ("o3", D),
             ("w1_1", FF * D), ("w2_1", FF * D)]
    at = 0
    for n, w in names:
        WCOLS[n] = (at, w)
        at += w
    return at


W_TOTAL = _pack_names()
W_FIRST = WCOLS["q0"][0]
W_SECOND = WCOLS["w1_0"][0]

BIAS = {n: i for i, n in enumerate(
    ["mod0", "mod1", "mod2", "mod3", "mod4", "mod5", "ln0", "ln1", "ln2", "ln3", "ln4", "ln5",
     "q0", "k0", "v0", "o0", "q1", "k1", "v1", "o1",
     "b1_0_0", "b1_0_1", "b1_0_2", "b1_0_3", "b2_0", "b1_1_0", "b1_1_1", "b1_1_2", "b1_1_3", "b2_1"])}
NB = len(BIAS)

CONST = {"ident": (0, P), "headmask": (P, H), "qmask": (P + H, 2 * GH),
         "cos": (P + H + 2 * GH, P), "sin": (P + H + 2 * GH + P, P)}
NCONST = P + H + 2 * GH + 2 * P

SHIFT_A, MULT_A, GATE_A, SHIFT_M, MULT_M, GATE_M, MULT_1, SHIFT_1, MULT_2, SHIFT_2, MULT_3, SHIFT_3 = range(12)
NV = 12

ATTN = [
    dict(eps=1e-6, mult=MULT_A, shift=SHIFT_A, cross=False, rope=False, gate=GATE_A, bias=True),
    dict(eps=1e-6, mult=None, shift=None, cross=True, rope=False, gate=None, bias=True),
    dict(eps=1e-5, mult=MULT_1, shift=SHIFT_1, cross=False, rope=True, gate=None, bias=False),
    dict(eps=1e-5, mult=MULT_2, shift=SHIFT_2, cross=True, rope=True, gate=None, bias=False),
]
MLP = [
    dict(eps=1e-6, mult=MULT_M, shift=SHIFT_M, gate=GATE_M, act="tanh"),
    dict(eps=1e-5, mult=MULT_3, shift=SHIFT_3, gate=None, act="erf"),
]


class Step:

    def __init__(self, kind, a=None, s=None, f=None, m=None, b=None, n=None, h=None, g=None, j=None, spec=None):
        self.kind = kind
        self.a = a
        self.s = s
        self.f = f
        self.m = m
        self.b = b
        self.n = n
        self.h = h
        self.g = g
        self.j = j
        self.spec = spec
        self.k = 0
        self.use = 0


def make_plan():
    steps = []

    def at(when, st):
        steps.append((when, len(steps), st))

    cells = [(b, n) for b in range(CB) for n in range(NG)]
    period = len(cells)
    for f in range(len(ATTN) * STREAMS):
        a, s, t = f // STREAMS, f % STREAMS, period * f
        who = dict(f=f, a=a, s=s)
        if a == 1:
            at(t - 33, Step("cln", **who))
            at(t - 31.5, Step("cT", **who))
        at(t - 31, Step("ln", spec=ATTN[a], **who))
        at(t - 29.5, Step("xT", spec=ATTN[a], **who))
        at(t - 28, Step("k", **who))
        at(t - 27.5, Step("q", **who))
        at(t - 26.6, Step("v", **who))
        for h in range(H):
            at(t - 25.4 + h, Step("kmask", h=h, **who))
        for i in range(period):
            at(t - 20.3 + i, Step("max", n=i // CB, b=i % CB, **who))
        at(t - 12.2, Step("mT", g=0, **who))
        at(t - 4.2, Step("mT", g=1, **who))
        for h in range(GH):
            at(t - 11.1 + h * 0.9, Step("qmask", h=h, **who))
            at(t - 3.3 + h * 0.5, Step("qmask", h=GH + h, **who))
        for i, (b, n) in enumerate(cells):
            at(t + i, Step("score", b=b, n=n, **who))
            at(t + i + 1.1, Step("value", b=b, n=n, **who))
        for b in range(CB):
            at(t + NG * b + NG + 0.2, Step("copy", b=b, **who))
            at(t + NG * b + NG + 1.2, Step("norm", b=b, **who))
        at(t + period + 3.3, Step("aT", **who))
        at(t + period + 4.6, Step("o", **who))
        at(t + period + 6.3, Step("yT", **who))
        if a % 2:
            layer, t = a // 2, t + period
            who = dict(m=layer * STREAMS + s, a=layer, s=s)
            at(t + 7.5, Step("ln", spec=MLP[layer], **who))
            at(t + 9, Step("xT", spec=MLP[layer], **who))
            for j in range(FF):
                at(t + 10.5, Step("h", j=j, **who))
            at(t + 12.3, Step("h2", **who))
            at(t + 14, Step("yT", **who))
            if layer == 1:
                at(t + 14, Step("store", **who))
    plan = [st for _, _, st in sorted(steps, key=lambda x: x[:2])]
    seen = {}
    for st in plan:
        st.k = seen.get(st.kind, 0)
        seen[st.kind] = st.k + 1
    uses, turned = [], 0
    for st in plan:
        st.use = len(uses)
        if st.kind == "xT":
            uses.append(("xnT_ready", CB * (st.k + 1)))
        elif st.kind == "cT":
            uses.append(("cnT_ready", st.k + 1))
        elif st.kind == "q":
            uses += ([("rope_read", 4 * rope_no(st.f) + 3), ("rope_read", 4 * rope_no(st.f) + 4)]
                     if ATTN[st.a]["rope"] else [("q_ready", 3 * (st.f + 1))])
        elif st.kind == "k":
            uses += ([("rope_read", 4 * rope_no(st.f) + 1), ("rope_read", 4 * rope_no(st.f) + 2)]
                     if ATTN[st.a]["rope"] else [("k_ready", 2 * (st.f + 1))])
        elif st.kind == "v":
            uses.append(("v_ready", st.k + 1))
        elif st.kind == "mT":
            uses.append(("maxT_ready", st.k + 1))
        elif st.kind == "aT":
            uses.append(("attT_ready", st.k + 1))
        elif st.kind == "h":
            uses.append(("hT_ready", st.k + 1))
        elif st.kind in ("o", "h2"):
            turned += 1
            uses.append(("y_ready", turned))
        elif st.kind == "yT":
            uses.append(("x_ready", st.k + 1))
    return plan, uses


def rope_no(f):
    return sum(ATTN[g // STREAMS]["rope"] for g in range(f))


def block_kernel(nc, weights, biases, consts, x_in, ctx_in, ctxT_in, out):
    plan, uses = make_plan()

    with ExitStack() as ctx:
        def sb(name, shape, dt=F32):
            return ctx.enter_context(nc.sbuf_tensor(name, shape, dt))

        def sem(name):
            return ctx.enter_context(nc.semaphore(name))

        W = sb("W", [P, W_TOTAL - W_FIRST])
        bias = sb("bias", [P, NB])
        cst = sb("cst", [P, NCONST])
        silu = sb("silu", [P, 3, B])
        vec = sb("vec", [P, B, NV])
        x = sb("x", [P, STREAMS, CB, D])
        craw = sb("craw", [P, STREAMS, CB, D])
        crawT = sb("crawT", [P, STREAMS, CB * NS_CTX])
        cnT = sb("cnT", [P, CB * NS_CTX])
        cn = sb("cn", [P, CB, D])
        stats = sb("stats", [P, 2, CB, 6])
        mv = sb("mv", [P, 2, CB, 2])
        vareps = sb("vareps", [P, 2, CB])
        rstd = sb("rstd", [P, 2, CB])
        minus_half = sb("minus_half", [P, CB])
        xn = sb("xn", [P, CB, D])
        xnT = sb("xnT", [P, 2, CT])
        ropeA = sb("ropeA", [P, CT])
        ropeB = sb("ropeB", [P, CT])
        QE = sb("QE", [P, 2, 2, CT])
        Qr = sb("Qr", [P, 2, CT], F32R)
        KE = sb("KE", [P, 3, 2, CT])
        Kd = sb("Kd", [P, 2 * HG, CT], F32R)
        Qd = sb("Qd", [P, 3, GH, CT])
        V = sb("V", [P, 3, CB, H, VW])
        mpadA = sb("mpadA", [P, CB, 96])
        mpadB = sb("mpadB", [P, CB, 32])
        PT = sb("PT", [P, 4, CT])
        AOs = sb("AOs", [P, 2, CT])
        rden = sb("rden", [P, 2, H])
        att = sb("att", [P, CB, D])
        attT = sb("attT", [P, CT])
        yT_sb = sb("yT_sb", [P, CT])
        hT = sb("hT", [P, FF, CT])

        ps_max = ctx.enter_context(nc.psum_tensor("ps_max", [P, 2, CT], F32))
        ps_sc = ctx.enter_context(nc.psum_tensor("ps_sc", [P, 2, CT], F32))
        ps_ao = ctx.enter_context(nc.psum_tensor("ps_ao", [P, CT], F32))
        ps_t = ctx.enter_context(nc.psum_tensor("ps_t", [P, CT], F32))
        ps_misc = ctx.enter_context(nc.psum_tensor("ps_misc", [P, 2, CT], F32))

        def w(name, j=0):
            at = WCOLS[name][0] - W_FIRST + j * D
            return W[:, at:at + D]

        first = Qd[:, :, :, :].rearrange("p a h t -> p (a h t)")[:, 0:W_FIRST]

        def w_first(name, j):
            return first[:, WCOLS[name][0] + j * D:WCOLS[name][0] + (j + 1) * D]

        def bcol(name):
            return bias[:, BIAS[name]:BIAS[name] + 1]

        def const(name):
            at, n = CONST[name]
            return cst[:, at:at + n]

        ident, headmask, qmask = const("ident"), const("headmask"), const("qmask")
        condT = first[:, WCOLS["condT"][0]:WCOLS["condT"][0] + B]

        names = ["x_in", "ctx_in", "small_in", "weights_in", "rest_in", "stored", "dve_chain",
                 "fixed_ready", "fixed_dve", "exp_done", "silu_done", "mod_products", "vec_ready",
                 "var_ready", "vareps_ready", "rstd_ready", "xn_ready", "cn_ready", "xnT_ready", "cnT_ready", "misc_filled",
                 "rope_read", "rope_chain", "q_ready", "q_roped", "k_ready", "k_roped", "v_ready", "kd_ready",
                 "max_scores", "max_taken", "maxT_ready", "qd_ready",
                 "scores_ready", "probs_ready", "values_done", "sums_copied", "sums_turned", "rden_ready",
                 "att_ready", "attT_ready", "hT_ready", "y_ready", "x_ready"]
        S = {n: sem(n) for n in names}
        FIXED = 6
        GROUPS = NG * CB

        def bank(n):
            return ps_misc[:, n % 2, :]

        def ns_of(st):
            return NS_CTX if ATTN[st.a]["cross"] else P

        feeds = {}
        update = {s: 0 for s in range(STREAMS)}
        normed = {s: 0 for s in range(STREAMS)}
        norms = [st for st in plan if st.kind in ("ln", "cln")]
        for number, st in enumerate(norms):
            st.norm_no = number
        for st in plan:
            if st.kind == "ln" and st.m is None:
                feeds[st.f] = st.k
            if st.kind == "ln" and st.m is not None:
                feeds["mlp", st.m] = st.k
            if st.kind in ("ln", "store"):
                st.after = update[st.s]
            if st.kind == "yT":
                update[st.s] = st.k + 1
                st.norms_before = normed[st.s]
            if st.kind == "ln":
                normed[st.s] = st.k + 1

        xT_use = {st.k: st.use for st in plan if st.kind == "xT"}
        v_after_cT = {st.s: st.f + 1 for st in plan if st.kind == "v" and st.a == 1}

        def key_source(st):
            if not ATTN[st.a]["cross"]:
                return xnT[:, feeds[st.f] % 2, :]
            return cnT[:, :] if st.a == 1 else crawT[:, st.s, :]

        def wait_keys(eng, f):
            if ATTN[f // STREAMS]["rope"]:
                eng.wait_ge(S["k_roped"], 2 * (rope_no(f) + 1))
            else:
                eng.wait_ge(S["k_ready"], 2 * (f + 1))

        def wait_queries(eng, f):
            if ATTN[f // STREAMS]["rope"]:
                eng.wait_ge(S["q_roped"], 3 * (rope_no(f) + 1))
            else:
                eng.wait_ge(S["q_ready"], 3 * (f + 1))

        with nc.Block() as block:
            @block.sync
            def _(sp):
                def load_x(s):
                    sp.dma_start(x[:, s, :, :].rearrange("p b f -> p (b f)"),
                                 x_in[:, s * CB * D:(s + 1) * CB * D]).then_inc(S["x_in"], 16)

                load_x(0)
                sp.dma_start(first, weights[:, 0:W_FIRST]).then_inc(S["small_in"], 16)
                sp.dma_start(W[:, 0:W_SECOND - W_FIRST], weights[:, W_FIRST:W_SECOND]).then_inc(S["weights_in"], 16)
                sp.wait_ge(S["x_in"], 16)
                for s in range(1, STREAMS):
                    load_x(s)
                    sp.wait_ge(S["x_in"], 16 * (s + 1))
                sp.dma_start(craw[0:NS_CTX, :, :, :].rearrange("p s b f -> p (s b f)"),
                             ctx_in).then_inc(S["ctx_in"], 16)
                sp.wait_ge(S["ctx_in"], 16)
                sp.dma_start(crawT[:, :, :].rearrange("p s t -> p (s t)"), ctxT_in).then_inc(S["ctx_in"], 16)
                sp.dma_start(W[:, W_SECOND - W_FIRST:W_TOTAL - W_FIRST],
                             weights[:, W_SECOND:W_TOTAL]).then_inc(S["rest_in"], 16)
                for st in plan:
                    if st.kind == "store":
                        sp.wait_ge(S["x_ready"], st.after)
                        sp.dma_start(out[:, st.s * CB * D:(st.s + 1) * CB * D],
                                     x[:, st.s, :, :].rearrange("p b f -> p (b f)")).then_inc(S["stored"], 16)
                sp.wait_ge(S["stored"], 16 * STREAMS)

            @block.vector
            def _(dve):
                chain = [0]

                def link(ins):
                    chain[0] += 1
                    return ins.then_inc(S["dve_chain"], 1)

                def linked():
                    dve.wait_ge(S["dve_chain"], chain[0])

                def norm(src, rows, dst, which, rstd_no, ready):
                    for b in range(CB):
                        link(dve.bn_stats(stats[0:rows, which, b, :], src[0:rows, b, :]))
                    linked()
                    for b in range(CB):
                        dve.bn_aggr(mv[0:rows, which, b, :],
                                    stats[0:rows, which, b, :]).then_inc(S["var_ready"], 1)
                    dve.wait_ge(S["rstd_ready"], rstd_no)
                    for b in range(CB):
                        dve.tensor_scalar(dst[0:rows, b, :], src[0:rows, b, :], mv[0:rows, which, b, 0:1],
                                          rstd[0:rows, which, b:b + 1], ALU.subtract,
                                          ALU.mult).then_inc(ready, 1)

                def rope(st, ns, dst_lo, dst_hi, ready, extra=None):
                    n = CB * ns
                    if st.kind == "q":
                        dve.wait_ge(S["k_roped"], 2 * (rope_no(st.f) + 1))
                    elif rope_no(st.f):
                        dve.wait_ge(S["q_roped"], 3 * rope_no(st.f))
                    dve.wait_ge(S["misc_filled"], st.use + 1)
                    for src, dst, table in ((bank(st.use), ropeA, "cos"), (bank(st.use + 1), ropeB, "sin")):
                        if table == "sin":
                            dve.wait_ge(S["misc_filled"], st.use + 2)
                        dve.tensor_tensor(dst[:, 0:n].rearrange("p (b t) -> p b t", b=CB),
                                          src[:, 0:n].rearrange("p (b t) -> p b t", b=CB),
                                          const(table)[:, None, 0:ns].to_broadcast([P, CB, ns]),
                                          ALU.mult).then_inc(S["rope_read"], 1)
                    dve.wait_ge(S["rope_read"], 4 * rope_no(st.f) + (2 if st.kind == "k" else 4))
                    dve.tensor_tensor(dst_lo, ropeA[0:64, 0:n], ropeB[0:64, 0:n], ALU.add).then_inc(ready, 1)
                    dve.tensor_tensor(dst_hi, ropeA[64:128, 0:n], ropeB[64:128, 0:n],
                                      ALU.add).then_inc(ready, 1)
                    if extra is not None:
                        dve.tensor_tensor(extra, ropeA[:, 0:n], ropeB[:, 0:n], ALU.add).then_inc(ready, 1)

                def modulation():
                    dve.wait_ge(S["mod_products"], 1)
                    for v in range(NV):
                        name = f"mod{v}" if v < 6 else f"ln{v - 6}"
                        one = 1.0 if v in (MULT_A, MULT_M, MULT_1, MULT_2, MULT_3) else 0.0
                        dve.tensor_scalar(vec[:, :, v], ps_sc[:, 0, v * B:(v + 1) * B], bcol(name), one,
                                          ALU.add, ALU.add).then_inc(S["vec_ready"], 1)

                dve.memset(ps_ao[:, :], 0.0).then_inc(S["fixed_dve"], 1)
                dve.wait_ge(S["exp_done"], 1)
                link(dve.tensor_scalar(silu[:, 1, :], silu[:, 0, :], 1.0, None, ALU.add))
                linked()
                link(dve.reciprocal(silu[:, 0, :], silu[:, 1, :]))
                linked()
                dve.tensor_tensor(silu[:, 2, :], condT, silu[:, 0, :], ALU.mult).then_inc(S["silu_done"], 1)
                for st in plan:
                    if st.kind == "ln":
                        if st.after:
                            dve.wait_ge(S["x_ready"], st.after)
                        else:
                            dve.wait_ge(S["x_in"], 16 * (st.s + 1))
                        if st.k:
                            dve.wait_ge(S["misc_filled"], xT_use[st.k - 1] + 1)
                        norm(x[:, st.s, :, :], P, xn, 0, st.norm_no + 1, S["xn_ready"])
                    elif st.kind == "cln":
                        dve.wait_ge(S["ctx_in"], 16)
                        if st.k:
                            dve.wait_ge(S["cnT_ready"], st.k)
                        norm(craw[:, st.s, :, :], NS_CTX, cn, 1, st.norm_no + 1, S["cn_ready"])
                    elif st.kind == "xT":
                        dve.wait_ge(S["misc_filled"], st.use + 1)
                        if st.k == 0:
                            modulation()
                            dve.wait_ge(S["vec_ready"], NV)
                        src, dst = bank(st.use), xnT[:, st.k % 2, :]
                        for b in range(CB):
                            o, i = dst[:, b * P:(b + 1) * P], src[:, b * P:(b + 1) * P]
                            if st.spec["mult"] is None:
                                dve.tensor_copy(o, i).then_inc(S["xnT_ready"], 1)
                            else:
                                c, m, sh = st.s * CB + b, st.spec["mult"], st.spec["shift"]
                                dve.tensor_scalar(o, i, vec[:, c, m:m + 1], vec[:, c, sh:sh + 1],
                                                  ALU.mult, ALU.add).then_inc(S["xnT_ready"], 1)
                    elif st.kind == "k" and ATTN[st.a]["rope"]:
                        n = CB * ns_of(st)
                        dve.wait_ge(S["scores_ready"], GROUPS * (st.f - 2))
                        rope(st, ns_of(st), KE[0:64, st.f % 3, 0, 0:n], KE[64:128, st.f % 3, 1, 0:n],
                             S["k_roped"])
                    elif st.kind == "q" and ATTN[st.a]["rope"]:
                        dve.wait_ge(S["max_scores"], GROUPS * (st.f - 1))
                        rope(st, P, QE[0:64, st.f % 2, 0, :], QE[64:128, st.f % 2, 1, :], S["q_roped"],
                             Qr[:, st.f % 2, :])
                    elif st.kind == "max":
                        ns = ns_of(st)
                        dve.wait_ge(S["max_scores"], st.k + 1)
                        dst = (mpadA[:, st.b, 64 + HG * st.n:64 + HG * st.n + HG] if st.n < NG // 2 else
                               mpadB[:, st.b, HG * (st.n - NG // 2):HG * (st.n - NG // 2) + HG])
                        dve.tensor_reduce(dst, ps_max[:, st.k % 2, 0:HG * ns].rearrange(
                            "p (h k) -> p h k", h=HG), AX_X, ALU.max, negate=True).then_inc(S["max_taken"], 1)
                    elif st.kind == "mT":
                        dve.wait_ge(S["misc_filled"], st.use + 1)
                        if st.g == 0:
                            ins = dve.tensor_copy(QE[64:96, st.f % 2, 0, :], bank(st.use)[64:96, :])
                        else:
                            ins = dve.tensor_copy(QE[0:32, st.f % 2, 1, :], bank(st.use)[0:32, :])
                        ins.then_inc(S["maxT_ready"], 1)
                    elif st.kind == "qmask":
                        g, j, q = st.h // GH, st.h % GH, 2 * st.f + st.h // GH
                        if j == 0:
                            wait_queries(dve, st.f)
                            dve.wait_ge(S["maxT_ready"], q + 1)
                            if q >= 3:
                                dve.wait_ge(S["scores_ready"], GROUPS * ((q - 3) // 2) + GROUPS - NG
                                            + NG // 2 * ((q - 3) % 2 + 1))
                        dve.tensor_scalar(Qd[:, q % 3, j, :], QE[:, st.f % 2, g, :], qmask[:, st.h:st.h + 1],
                                          None, ALU.mult).then_inc(S["qd_ready"], 1)
                    elif st.kind == "norm":
                        turned = ps_t[:, :].rearrange("p (n c r) -> p (n c) r", n=NG, c=HG)
                        dve.wait_ge(S["sums_turned"], st.k + 1)
                        dve.reciprocal(rden[:, st.k % 2, :], turned[:, :, HD]).then_inc(S["rden_ready"], 1)
                        dve.wait_ge(S["rden_ready"], st.k + 1)
                        if st.b == 0 and st.f:
                            dve.wait_ge(S["attT_ready"], st.f)
                        dve.tensor_tensor(att[:, st.b, :].rearrange("p (h d) -> p h d", h=H),
                                          turned[:, :, 0:HD],
                                          rden[:, st.k % 2, :][:, :, None].to_broadcast([P, H, HD]),
                                          ALU.mult).then_inc(S["att_ready"], 1)
                    elif st.kind in ("o", "h2"):
                        if st.kind == "o":
                            gate = ATTN[st.a]["gate"]
                            add = bcol(f"o{st.a}") if ATTN[st.a]["bias"] else None
                        else:
                            gate, add = MLP[st.a]["gate"], bcol(f"b2_{st.a}")
                        dve.wait_ge(S["misc_filled"], st.use + 1)
                        src = bank(st.use)
                        if gate is not None:
                            for b in range(CB):
                                c = st.s * CB + b
                                ins = dve.tensor_scalar(yT_sb[:, b * P:(b + 1) * P], src[:, b * P:(b + 1) * P],
                                                        add, vec[:, c, gate:gate + 1], ALU.add, ALU.mult)
                        elif add is not None:
                            ins = dve.tensor_scalar(yT_sb[:, :], src, add, None, ALU.add)
                        else:
                            ins = dve.tensor_copy(yT_sb[:, :], src)
                        ins.then_inc(S["y_ready"], 1)
                    elif st.kind == "yT":
                        dve.wait_ge(S["misc_filled"], st.use + 1)
                        dve.wait_ge(S["xn_ready"], CB * st.norms_before)
                        flat = x[:, st.s, :, :].rearrange("p b f -> p (b f)")
                        dve.tensor_tensor(flat, bank(st.use), flat, ALU.add).then_inc(S["x_ready"], 1)

            @block.gpsimd
            def _(pool):
                for tile, value in ((minus_half[:, :], -0.5), (mpadA[:, :, :], 0.0), (mpadB[:, :, :], 0.0),
                                    (KE[:, :, :, :], 1.0), (QE[:, :, :, :], 0.0), (V[:, :, :, :, :], 1.0)):
                    pool.memset(tile, value).then_inc(S["fixed_ready"], 1)
                for st in norms:
                    rows, which, eps = (P, 0, st.spec["eps"]) if st.kind == "ln" else (NS_CTX, 1, 1e-6)
                    pool.wait_ge(S["var_ready"], CB * (st.norm_no + 1))
                    pool.tensor_scalar(vareps[0:rows, which, :], mv[0:rows, which, :, 1], eps, None,
                                       ALU.add).then_inc(S["vareps_ready"], 1)
                    pool.wait_ge(S["vareps_ready"], st.norm_no + 1)
                    pool.tensor_tensor(rstd[0:rows, which, :], vareps[0:rows, which, :],
                                       minus_half[0:rows, :], ALU.pow).then_inc(S["rstd_ready"], 1)

            @block.scalar
            def _(act):
                act.dma_start(bias[:, :], biases).then_inc(S["small_in"], 16)
                act.dma_start(cst[:, :], consts).then_inc(S["small_in"], 16)
                act.wait_ge(S["small_in"], 48)
                act.activation(silu[:, 0, :], condT, ACT.Exp, scale=-1.0).then_inc(S["exp_done"], 1)
                for st in plan:
                    if st.kind == "cT":
                        act.wait_ge(S["misc_filled"], st.use + 1)
                        if st.k:
                            act.wait_ge(S["v_ready"], v_after_cT[st.k - 1])
                        act.activation(cnT[:, :], bank(st.use)[:, 0:CB * NS_CTX],
                                       ACT.Copy).then_inc(S["cnT_ready"], 1)
                    elif st.kind == "k" and not ATTN[st.a]["rope"]:
                        n = CB * ns_of(st)
                        act.wait_ge(S["misc_filled"], st.use + 1)
                        if st.f >= 3:
                            act.wait_ge(S["scores_ready"], GROUPS * (st.f - 2))
                        elif st.f == 0:
                            act.wait_ge(S["fixed_ready"], FIXED)
                        for g in range(2):
                            r = slice(64 * g, 64 * g + 64)
                            act.activation(KE[r, st.f % 3, g, 0:n], bank(st.use)[r, 0:n], ACT.Identity,
                                           bias=bcol(f"k{st.a}")[r, :]).then_inc(S["k_ready"], 1)
                    elif st.kind == "q" and not ATTN[st.a]["rope"]:
                        act.wait_ge(S["misc_filled"], st.use + 1)
                        if st.f >= 2:
                            act.wait_ge(S["qd_ready"], H * (st.f - 1))
                            act.wait_ge(S["max_scores"], GROUPS * (st.f - 1))
                        for g in range(2):
                            r = slice(64 * g, 64 * g + 64)
                            act.activation(QE[r, st.f % 2, g, :], bank(st.use)[r, :], ACT.Identity,
                                           bias=bcol(f"q{st.a}")[r, :]).then_inc(S["q_ready"], 1)
                        act.activation(Qr[:, st.f % 2, :], bank(st.use), ACT.Identity,
                                       bias=bcol(f"q{st.a}")).then_inc(S["q_ready"], 1)
                    elif st.kind == "v":
                        ns = ns_of(st)
                        act.wait_ge(S["misc_filled"], st.use + 1)
                        if st.f >= 3:
                            act.wait_ge(S["values_done"], GROUPS * (st.f - 2))
                        act.activation(V[0:ns, st.f % 3, :, :, 0:HD],
                                       bank(st.use)[0:ns, :].rearrange("p (b h d) -> p b h d", b=CB, h=H),
                                       ACT.Copy).then_inc(S["v_ready"], 1)
                    elif st.kind == "kmask":
                        n = CB * ns_of(st)
                        group = NG * st.f + st.h // HG
                        if st.h == 0:
                            wait_keys(act, st.f)
                        if st.h % HG == 0 and group >= 2:
                            act.wait_ge(S["max_scores"], CB * (group - 1))
                        act.activation(Kd[:, st.h % (2 * HG), 0:n], KE[:, st.f % 3, st.h // GH, 0:n], ACT.Copy,
                                       scale=headmask[:, st.h:st.h + 1]).then_inc(S["kd_ready"], 1)
                    elif st.kind == "score":
                        ns = ns_of(st)
                        act.wait_ge(S["scores_ready"], st.k + 1)
                        if st.k >= 4:
                            act.wait_ge(S["values_done"], st.k - 3)
                        act.activation(PT[0:ns, st.k % 4, :], ps_sc[0:ns, st.k % 2, :], ACT.Exp,
                                       scale=SCALE).then_inc(S["probs_ready"], 1)
                    elif st.kind == "copy":
                        act.wait_ge(S["values_done"], HG * (st.k + 1))
                        if st.k >= 2:
                            act.wait_ge(S["sums_turned"], st.k - 1)
                        act.activation(AOs[:, st.k % 2, :], ps_ao[:, :], ACT.Copy).then_inc(S["sums_copied"], 1)
                    elif st.kind == "aT":
                        act.wait_ge(S["misc_filled"], st.use + 1)
                        if ATTN[st.a]["bias"]:
                            ins = act.activation(attT[:, :], bank(st.use), ACT.Identity, bias=bcol(f"v{st.a}"))
                        else:
                            ins = act.activation(attT[:, :], bank(st.use), ACT.Copy)
                        ins.then_inc(S["attT_ready"], 1)
                    elif st.kind == "h":
                        act.wait_ge(S["misc_filled"], st.use + 1)
                        act.activation(hT[:, st.j, :], bank(st.use),
                                       ACT.Gelu_apprx_tanh if MLP[st.a]["act"] == "tanh" else ACT.Gelu,
                                       bias=bcol(f"b1_{st.a}_{st.j}")).then_inc(S["hT_ready"], 1)

            @block.tensor
            def _(pe):
                filled = [0]

                def fill(n):
                    if n >= 2:
                        pe.wait_ge(S[uses[n - 2][0]], uses[n - 2][1])

                def turn(src, use, rows=P):
                    for b in range(CB):
                        last = pe.transpose(bank(use)[:, b * rows:(b + 1) * rows], src[0:rows, b, :],
                                            ident[0:rows, 0:rows])
                    last.then_inc(S["misc_filled"], 1)

                pe.wait_ge(S["silu_done"], 1)
                for v in range(NV):
                    lhs, rhs = ((w_first("mod", v), silu[:, 2, :]) if v < 6 else
                                (w_first("ln", v - 6), condT))
                    last = pe.matmul(ps_sc[:, 0, v * B:(v + 1) * B], lhs, rhs, start=True, stop=True)
                last.then_inc(S["mod_products"], 1)
                for st in plan:
                    if st.kind == "xT":
                        fill(st.use)
                        pe.wait_ge(S["xn_ready"], CB * (st.k + 1))
                        turn(xn, st.use)
                    elif st.kind == "cT":
                        fill(st.use)
                        pe.wait_ge(S["cn_ready"], CB * (st.k + 1))
                        turn(cn, st.use, NS_CTX)
                    elif st.kind in ("k", "q"):
                        n = CB * (ns_of(st) if st.kind == "k" else P)
                        if st.kind == "k":
                            if st.a == 0 or st.a == 2:
                                pe.wait_ge(S["xnT_ready"], CB * (feeds[st.f] + 1))
                            elif st.a == 1:
                                pe.wait_ge(S["cnT_ready"], st.s + 1)
                            else:
                                pe.wait_ge(S["ctx_in"], 32)
                            if st.f == 0:
                                pe.wait_ge(S["weights_in"], 16)
                            src = key_source(st)
                        else:
                            pe.wait_ge(S["xnT_ready"], CB * (feeds[st.f] + 1))
                            src = xnT[:, feeds[st.f] % 2, :]
                        forms = ["", "s"] if ATTN[st.a]["rope"] else [""]
                        for i, form in enumerate(forms):
                            fill(st.use + i)
                            pe.matmul(bank(st.use + i)[:, 0:n], w(f"{st.kind}{st.a}{form}"), src[:, 0:n],
                                      start=True, stop=True).then_inc(S["misc_filled"], 1)
                    elif st.kind == "v":
                        ns = ns_of(st)
                        fill(st.use)
                        src = key_source(st)
                        for b in range(CB):
                            last = pe.matmul(bank(st.use)[0:ns, b * D:(b + 1) * D], src[:, b * ns:(b + 1) * ns],
                                             w(f"v{st.a}"), start=True, stop=True)
                        last.then_inc(S["misc_filled"], 1)
                    elif st.kind == "max":
                        ns = ns_of(st)
                        if st.b == 0:
                            pe.wait_ge(S["kd_ready"], H * st.f + HG * (st.n + 1))
                        if st.b == 0 and st.n == 0:
                            wait_queries(pe, st.f)
                        if st.k >= 2:
                            pe.wait_ge(S["max_taken"], st.k - 1)
                        pe.matmul(ps_max[:, st.k % 2, 0:HG * ns], Qr[:, st.f % 2, st.b * P:(st.b + 1) * P],
                                  Kd[:, HG * (st.n % 2):HG * (st.n % 2) + HG, st.b * ns:(st.b + 1) * ns],
                                  start=True, stop=True).then_inc(S["max_scores"], 1)
                    elif st.kind == "mT":
                        fill(st.use)
                        pe.wait_ge(S["max_taken"], GROUPS * st.f + GROUPS // 2 * (st.g + 1))
                        src, rows = (mpadA, 96) if st.g == 0 else (mpadB, 32)
                        for b in range(CB):
                            last = pe.transpose(bank(st.use)[0:rows, b * P:(b + 1) * P], src[:, b, :], ident)
                        last.then_inc(S["misc_filled"], 1)
                    elif st.kind == "score":
                        ns, g = ns_of(st), st.n // (NG // 2)
                        if st.b == 0:
                            pe.wait_ge(S["qd_ready"], H * st.f + HG * (st.n + 1))
                        if st.b == 0 and st.n == 0:
                            wait_keys(pe, st.f)
                        if st.k >= 2:
                            pe.wait_ge(S["probs_ready"], st.k - 1)
                        third, j = (2 * st.f + g) % 3, HG * (st.n % (NG // 2))
                        pe.matmul(ps_sc[0:ns, st.k % 2, :], KE[:, st.f % 3, g, st.b * ns:(st.b + 1) * ns],
                                  Qd[:, third, j:j + HG, st.b * P:(st.b + 1) * P],
                                  start=True, stop=True).then_inc(S["scores_ready"], 1)
                    elif st.kind == "value":
                        ns = ns_of(st)
                        pe.wait_ge(S["probs_ready"], st.k + 1)
                        if st.b == 0 and st.n == 0:
                            pe.wait_ge(S["v_ready"], st.f + 1)
                        if st.n == 0 and st.k:
                            pe.wait_ge(S["sums_copied"], st.k // NG)
                        for c in range(HG):
                            last = pe.matmul(ps_ao[32 * c:32 * c + VW, st.n * P:(st.n + 1) * P],
                                             V[0:ns, st.f % 3, st.b, HG * st.n + c, :],
                                             PT[0:ns, st.k % 4, c * P:(c + 1) * P], start=True, stop=True)
                        last.then_inc(S["values_done"], 1)
                    elif st.kind == "norm":
                        pe.wait_ge(S["sums_copied"], st.k + 1)
                        if st.k:
                            pe.wait_ge(S["att_ready"], st.k)
                        for n in range(NG):
                            last = pe.transpose(ps_t[:, n * P:(n + 1) * P], AOs[:, st.k % 2, n * P:(n + 1) * P],
                                                ident)
                        last.then_inc(S["sums_turned"], 1)
                    elif st.kind == "aT":
                        fill(st.use)
                        pe.wait_ge(S["att_ready"], CB * (st.f + 1))
                        turn(att, st.use)
                    elif st.kind == "o":
                        fill(st.use)
                        pe.wait_ge(S["attT_ready"], st.k + 1)
                        pe.matmul(bank(st.use), w(f"o{st.a}"), attT[:, :], start=True,
                                  stop=True).then_inc(S["misc_filled"], 1)
                    elif st.kind == "h":
                        fill(st.use)
                        pe.wait_ge(S["xnT_ready"], CB * (feeds["mlp", st.m] + 1))
                        if st.k == 0:
                            pe.wait_ge(S["rest_in"], 16)
                        pe.matmul(bank(st.use), w(f"w1_{st.a}", st.j), xnT[:, feeds["mlp", st.m] % 2, :],
                                  start=True, stop=True).then_inc(S["misc_filled"], 1)
                    elif st.kind == "h2":
                        fill(st.use)
                        pe.wait_ge(S["hT_ready"], FF * (st.m + 1))
                        for j in range(FF):
                            last = pe.matmul(bank(st.use), w(f"w2_{st.a}", j), hT[:, j, :], start=(j == 0),
                                             stop=(j == FF - 1))
                        last.then_inc(S["misc_filled"], 1)
                    elif st.kind == "yT":
                        fill(st.use)
                        pe.wait_ge(S["y_ready"], st.k + 1)
                        for b in range(CB):
                            last = pe.transpose(bank(st.use)[:, b * P:(b + 1) * P], yT_sb[:, b * P:(b + 1) * P],
                                                ident)
                        last.then_inc(S["misc_filled"], 1)


def _constants():
    c = np.zeros((P, NCONST), np.float32)
    p = np.arange(P)
    at = CONST["ident"][0]
    c[p, at + p] = 1.0
    c[p, CONST["headmask"][0] + p // HD] = 1.0
    at = CONST["qmask"][0]
    for g in range(2):
        for j in range(GH):
            lo = 64 * g + HD * j
            c[lo:lo + HD, at + GH * g + j] = 1.0
            c[64 * (1 - g) + j, at + GH * g + j] = 1.0
    half = HD // 2
    inv = (1.0 / np.float32(10000.0) ** (np.arange(half, dtype=np.float32) / half)).astype(np.float32)
    ang = (np.arange(P, dtype=np.float32)[None, :] * inv[p % half][:, None]).astype(np.float32)
    at = CONST["cos"][0]
    c[:, at:at + P] = np.cos(ang)
    at = CONST["sin"][0]
    c[:, at:at + P] = np.sin(ang) * np.where(p % HD < half, -1.0, 1.0)[:, None].astype(np.float32)
    return c


def kernel(**inputs):
    import concourse.bacc as _bacc
    from concourse.bass_utils import run_bass_kernel_spmd as _run

    i = {n: np.asarray(a) for n, a in inputs.items()}
    L0, L1 = "L0_xcond_", "L1_xcond_"

    def blocks(a):
        return a.reshape(-1, P, a.shape[1]).transpose(1, 0, 2).reshape(P, -1)

    swap = (np.arange(D) // HD) * HD + (np.arange(D) + HD // 2) % HD
    qkv0, kvc0 = i[L0 + "W_qkv"], i[L0 + "W_kvc"]
    qkv1 = i[L1 + "qkv_w"].T
    parts = {
        "mod": i[L0 + "W_mod"],
        "ln": np.concatenate([i[L1 + f"ln{n}_w"].T for n in (1, 2, 3)], axis=1),
        "condT": i["cond_1024"].T,
        "q0": qkv0[:, 0:D], "k0": qkv0[:, D:2 * D], "v0": qkv0[:, 2 * D:], "o0": i[L0 + "W_proj"],
        "q1": i[L0 + "W_qc"], "k1": kvc0[:, 0:D], "v1": kvc0[:, D:], "o1": i[L0 + "W_cproj"],
        "w1_0": i[L0 + "W_mlp1"], "w2_0": blocks(i[L0 + "W_mlp2"]),
        "q2": qkv1[:, 0:D], "q2s": qkv1[:, 0:D][:, swap], "k2": qkv1[:, D:2 * D],
        "k2s": qkv1[:, D:2 * D][:, swap], "v2": qkv1[:, 2 * D:], "o2": i[L1 + "sa_out_w"].T,
        "q3": i[L1 + "q_w"].T, "q3s": i[L1 + "q_w"].T[:, swap], "k3": i[L1 + "k_w"].T,
        "k3s": i[L1 + "k_w"].T[:, swap], "v3": i[L1 + "v_w"].T, "o3": i[L1 + "ca_out_w"].T,
        "w1_1": i[L1 + "ffn_w1"].T, "w2_1": blocks(i[L1 + "ffn_w2"].T),
    }
    weights = np.concatenate([parts[n] for n in WCOLS], axis=1)
    bq = i[L0 + "b_qkv"].reshape(3, D)
    bkv = i[L0 + "b_kvc"].reshape(2, D)
    biases = np.concatenate([
        i[L0 + "b_mod"].reshape(6, D), i[L1 + "ln1_b"].reshape(2, D), i[L1 + "ln2_b"].reshape(2, D),
        i[L1 + "ln3_b"].reshape(2, D), bq, i[L0 + "b_proj"][None], i[L0 + "b_qc"][None], bkv,
        i[L0 + "b_cproj"][None], i[L0 + "b_mlp1"].reshape(FF, D), i[L0 + "b_mlp2"][None],
        i[L1 + "ffn_b1"].reshape(FF, D), i[L1 + "ffn_b2"][None]], axis=0).T
    arrays = {
        "weights": weights, "biases": biases, "consts": _constants(),
        "x_in": i["x"].transpose(1, 0, 2).reshape(P, B * D),
        "ctx_in": i["ctx_1024"].transpose(1, 0, 2).reshape(NS_CTX, B * D),
        "ctxT_in": i["ctx_1024"].transpose(2, 0, 1).reshape(D, B * NS_CTX),
    }
    arrays = {n: np.ascontiguousarray(a) for n, a in arrays.items()}
    nc = _bacc.Bacc("TRN2", target_bir_lowering=False, num_devices=1)
    args = [nc.dram_tensor(n, a.shape, F32, kind="ExternalInput").ap() for n, a in arrays.items()]
    out = nc.dram_tensor("out", (P, B * D), F32, kind="ExternalOutput").ap()
    block_kernel(nc, *args, out)
    r = _run(nc, [arrays], core_ids=[0])
    return np.ascontiguousarray(np.asarray(r.results[0]["out"]).reshape(P, B, D).transpose(1, 0, 2))
```

```python
from contextlib import ExitStack

import numpy as np

import concourse.bass as bass
from concourse import mybir

ALU = mybir.AluOpType
ACT = mybir.ActivationFunctionType
AX_X = mybir.AxisListType.X
F32 = mybir.dt.float32
F32R = mybir.dt.float32r

P = 128
D = 128
B = 16
NS_CTX = 120
H = 16
HD = D // H
SCALE = HD ** -0.5
CB = 4
CT = CB * P
STREAMS = B // CB
HG = 4
NG = H // HG
GH = H // 2
GP = NG // 2
SPLIT = 3
SR = SPLIT * HD
SROWS = HG * SR
FF = 4
BANKS = 3
VW = HD + 1

WCOLS = {}


def _pack_names():
    names = [("mod", 6 * D), ("ln", 6 * D), ("condT", B),
             ("q0", D), ("k0", D), ("v0", D), ("o0", D),
             ("q1", D), ("k1", D), ("v1", D), ("o1", D), ("w1_0", FF * D), ("w2_0", FF * D),
             ("q2", D), ("q2s", D), ("k2", D), ("k2s", D), ("v2", D), ("o2", D),
             ("q3", D), ("q3s", D), ("k3", D), ("k3s", D), ("v3", D), ("o3", D),
             ("w1_1", FF * D), ("w2_1", FF * D)]
    at = 0
    for n, w in names:
        WCOLS[n] = (at, w)
        at += w
    return at


W_TOTAL = _pack_names()
W_FIRST = WCOLS["q0"][0]
W_SECOND = WCOLS["w1_0"][0]

BIAS = {n: i for i, n in enumerate(
    ["mod0", "mod1", "mod2", "mod3", "mod4", "mod5", "ln0", "ln1", "ln2", "ln3", "ln4", "ln5",
     "q0", "k0", "v0", "o0", "q1", "k1", "v1", "o1",
     "b1_0_0", "b1_0_1", "b1_0_2", "b1_0_3", "b2_0", "b1_1_0", "b1_1_1", "b1_1_2", "b1_1_3", "b2_1"])}
NB = len(BIAS)

CONST = {"ident": (0, P), "cos": (P, P), "sin": (2 * P, P)}
NCONST = 3 * P

SHIFT_A, MULT_A, GATE_A, SHIFT_M, MULT_M, GATE_M, MULT_1, SHIFT_1, MULT_2, SHIFT_2, MULT_3, SHIFT_3 = range(12)
NV = 12

ATTN = [
    dict(eps=1e-6, mult=MULT_A, shift=SHIFT_A, cross=False, rope=False, gate=GATE_A, bias=True),
    dict(eps=1e-6, mult=None, shift=None, cross=True, rope=False, gate=None, bias=True),
    dict(eps=1e-5, mult=MULT_1, shift=SHIFT_1, cross=False, rope=True, gate=None, bias=False),
    dict(eps=1e-5, mult=MULT_2, shift=SHIFT_2, cross=True, rope=True, gate=None, bias=False),
]
MLP = [
    dict(eps=1e-6, mult=MULT_M, shift=SHIFT_M, gate=GATE_M, act="tanh"),
    dict(eps=1e-5, mult=MULT_3, shift=SHIFT_3, gate=None, act="erf"),
]


class Step:

    def __init__(self, kind, a=None, s=None, f=None, m=None, b=None, n=None, h=None, g=None, j=None, spec=None):
        self.kind = kind
        self.a = a
        self.s = s
        self.f = f
        self.m = m
        self.b = b
        self.n = n
        self.h = h
        self.g = g
        self.j = j
        self.spec = spec
        self.k = 0
        self.use = 0


T = dict(
    ln=(-35.5, -34.5, -34.5, -34.5),
    xT=(-32.5, -31.5, -31.5, -31.5),
    k=(-30.5, -30.5, -30.5, -30.5),
    q=(-29.2, -29.2, -29.2, -29.2),
    v=(-28.7, -28.0, -27.5, -28.0),
    kmask=(-29.9, -29.4, -29.4, -29.5),
    kstep=(0.15, 0.15, 0.15, 0.15),
    max=(-24.8, -24.3, -24.3, -24.3),
    mstep=(1.05, 1.05, 1.05, 1.05),
    mT=(-7.8, -7.3, -7.3, -7.3),
    kload=(-15, -15, -15, -15),
    qload=(-15.2, -15.1, -15.2, -15.2),
    mload=(-6.0, -5.5, -5.5, -5.5),
    copy=(0.4, 0.4, 0.3, 0.4),
    norm=(4.0, 3.0, 3.0, 3.0),
    aT=(4.8, 4.8, 4.8, 4.8),
    o=(5.7, 5.7, 5.7, 5.7),
    yT=(8.9, 8.9, 8.9, 8.9),
    mln=(7.2, 7.9),
    mxT=(8.5, 10.5),
    mh=(9.8, 11.8),
    mh2=(10.9, 12.9),
    myT=(12.1, 13.6),
    bias=(-7.5, -7.5, -7.5, -7.5),
    apply=(0.8, 0.8, 0.8, 0.8),
    kstore=(1.1, 0.1, 1.1, 0.1),
    qstore=(0.1, 0.1, 0.1, 0.1),
    mstore=(0.1, 0.1, 0.1, 0.1),
    msecond=(0.1, 0.1, 0.1, 0.1),
    qsecond=(8, 8, 8, 8),
    klo=(1.3, 1.3, 1.3, 1.4),
    qlo=(1.4, 1.4, 1.4, 1.4),
    khi=(0.9, -0.2, 0.3, 1.3),
    qhi=(0.8, -0.2, 0.3, 0.3),
    value=(1.1, 1.1, 1.1, 1.1),
    cln=(-36.1, -35.85, -36.1, -36.1),
    cT=(-34.5, -34.25, -34.5, -34.5),
    mapply=(1.0, 1.0),
)


def make_plan():
    steps = []

    def at(when, st):
        steps.append((when, len(steps), st))

    cells = [(b, n) for g in range(2) for b in range(CB) for n in range(GP * g, GP * g + GP)]
    period = len(cells)
    for f in range(len(ATTN) * STREAMS):
        a, s, t = f // STREAMS, f % STREAMS, period * f
        who = dict(f=f, a=a, s=s)
        if a == 1:
            at(t + T["cln"][a] - T["apply"][a], Step("cstats", **who))
            at(t + T["cln"][a], Step("cln", **who))
            at(t + T["cT"][a], Step("cT", **who))
        at(t + T["ln"][a] - T["apply"][a], Step("stats", spec=ATTN[a], **who))
        at(t + T["ln"][a], Step("ln", spec=ATTN[a], **who))
        at(t + T["xT"][a], Step("xT", spec=ATTN[a], **who))
        at(t + T["k"][a], Step("k", **who))
        at(t + T["q"][a], Step("q", **who))
        for x in "kq":
            at(t + T[x][a] + T[x + "hi"][a], Step(x + "hi", **who))
            at(t + T[x][a] + T[x + "lo"][a], Step(x + "lo", **who))
            at(t + T[x][a] + T[x + "lo"][a] + T[x + "store"][a], Step(x + "store", **who))
        at(t + T["v"][a], Step("v", **who))
        for h in range(H):
            at(t + T["kmask"][a] + h * T["kstep"][a], Step("kmask", h=h, **who))
        for i in range(period):
            at(t + T["max"][a] + i * T["mstep"][a], Step("max", n=i // CB, b=i % CB, **who))
        at(t + T["mT"][a], Step("mT", **who))
        at(t + T["mT"][a] + T["mstore"][a], Step("mstore", **who))
        at(t + T["kload"][a], Step("kload", **who))
        for g in range(2):
            at(t + T["qload"][a] + T["qsecond"][a] * g, Step("qload", g=g, **who))
            at(t + T["mload"][a] + T["msecond"][a] * g, Step("mload", g=g, **who))
        for i, (b, n) in enumerate(cells):
            at(t + i, Step("score", b=b, n=n, **who))
            at(t + i + T["value"][a], Step("value", b=b, n=n, **who))
        for i in range(CB):
            bank = dict(g=i // 2, b=i % 2 * 2)
            at(t + NG * i + NG + T["copy"][a], Step("copy", **bank, **who))
            at(t + NG * i + NG + T["norm"][a], Step("norm", **bank, **who))
        at(t + period + T["aT"][a], Step("aT", **who))
        if ATTN[a]["gate"] is None:
            if ATTN[a]["bias"]:
                at(t + T["bias"][a], Step("bias", **who))
            at(t + period + T["o"][a], Step("out", **who))
        else:
            at(t + period + T["o"][a], Step("o", **who))
            at(t + period + T["yT"][a], Step("yT", **who))
        if a % 2:
            layer, t = a // 2, t + period
            who = dict(m=layer * STREAMS + s, a=layer, s=s)
            at(t + T["mln"][layer] - T["mapply"][layer], Step("stats", spec=MLP[layer], **who))
            at(t + T["mln"][layer], Step("ln", spec=MLP[layer], **who))
            at(t + T["mxT"][layer], Step("xT", spec=MLP[layer], **who))
            for j in range(FF):
                at(t + T["mh"][layer], Step("h", j=j, **who))
            if MLP[layer]["gate"] is None:
                at(t + T["mh"][layer] - 0.1, Step("bias", **who))
                at(t + T["mh2"][layer], Step("out", **who))
                at(t + T["mh2"][layer] + 0.1, Step("store", **who))
            else:
                at(t + T["mh2"][layer], Step("h2", **who))
                at(t + T["myT"][layer], Step("yT", **who))
    plan = [st for _, _, st in sorted(steps, key=lambda x: x[:2])]
    for s in range(STREAMS):
        done, unit = 0, None
        for st in plan:
            if st.s == s and st.kind == "stats":
                assert done == (st.a + st.a // 2 if st.m is None else 3 * st.a + 2), "a norm before its input"
            done += st.s == s and st.kind in ("yT", "out")
            if st.s == s and st.kind in ("ln", "bias", "yT", "out"):
                assert (st.a, st.m) == unit or st.kind == "ln", "a bias or an update before its norm"
                unit = (st.a, st.m)
    order = [st.kind for st in plan if st.kind in ("stats", "ln")]
    assert order == ["stats", "ln"] * (len(order) // 2), "statistics overwritten"
    order = [st.kind for st in plan if st.kind in ("cstats", "cln")]
    assert order == ["cstats", "cln"] * (len(order) // 2), "statistics overwritten"
    seen = {}
    for st in plan:
        st.k = seen.get(st.kind, 0)
        seen[st.kind] = st.k + 1
    uses, turned, updates = [], 0, 0
    for st in plan:
        st.use = len(uses)
        if st.kind == "xT":
            uses.append(("xnT_ready", CB * (st.k + 1)))
        elif st.kind == "cT":
            uses.append(("cnT_ready", st.k + 1))
        elif st.kind == "q":
            uses += ([("rope_read", 4 * rope_no(st.f) + 3), ("rope_read", 4 * rope_no(st.f) + 4)]
                     if ATTN[st.a]["rope"] else [("q_low", st.f + 1)])
        elif st.kind == "k":
            uses += ([("rope_read", 4 * rope_no(st.f) + 1), ("rope_read", 4 * rope_no(st.f) + 2)]
                     if ATTN[st.a]["rope"] else [("k_low", st.f + 1)])
        elif st.kind == "v":
            uses.append(("v_ready", st.k + 1))
        elif st.kind == "mT":
            uses.append(("maxT_ready", st.k + 1))
        elif st.kind == "aT":
            uses.append(("attT_ready", st.k + 1))
        elif st.kind == "h":
            uses.append(("hT_ready", st.k + 1))
        elif st.kind in ("o", "h2"):
            turned += 1
            uses.append(("y_ready", turned))
        elif st.kind == "norm":
            uses.append(("att_ready", 2 * (st.k + 1)))
        elif st.kind in ("yT", "out"):
            updates += 1
            st.update = updates
            uses.append(("x_ready", updates))
    return plan, uses


def rope_no(f):
    return sum(ATTN[g // STREAMS]["rope"] for g in range(f))


def block_kernel(nc, weights, biases, consts, x_in, ctx_in, ctxT_in, rows_in, q_mem, k_mem, m_mem, out):
    plan, uses = make_plan()

    with ExitStack() as ctx:
        def sb(name, shape, dt=F32):
            return ctx.enter_context(nc.sbuf_tensor(name, shape, dt))

        def sem(name):
            return ctx.enter_context(nc.semaphore(name))

        W = sb("W", [P, W_TOTAL - W_FIRST])
        bias = sb("bias", [P, NB])
        bias_rows = sb("bias_rows", [P, 2, D])
        cst = sb("cst", [P, NCONST])
        silu = sb("silu", [P, 3, B])
        vec = sb("vec", [P, B, NV])
        x = sb("x", [P, STREAMS, CB, D])
        craw = sb("craw", [P, STREAMS, CB, D])
        crawT = sb("crawT", [P, STREAMS, CB * NS_CTX])
        cnT = sb("cnT", [P, CB * NS_CTX])
        cn = sb("cn", [P, CB, D])
        stats = sb("stats", [P, 2, CB, 6])
        mv = sb("mv", [P, 2, CB, 2])
        vareps = sb("vareps", [P, 2, CB])
        rstd = sb("rstd", [P, 2, CB])
        minus_half = sb("minus_half", [P, CB])
        xn = sb("xn", [P, CB, D])
        xnT = sb("xnT", [P, 2, CT])
        ropeA = sb("ropeA", [P, 2, CT])
        ropeB = sb("ropeB", [P, CT])
        Qh = sb("Qh", [P, 2, CT], F32R)
        Ql = sb("Ql", [P, CT], F32R)
        Kh = sb("Kh", [P, 2, CT], F32R)
        Kl = sb("Kl", [P, CT], F32R)
        Kd = sb("Kd", [P, H, CT], F32R)
        Ks = sb("Ks", [SROWS + 1, 2, NG, CT], F32R)
        Qd = sb("Qd", [SROWS + 1, 3, GP, HG, CT], F32R)
        V = sb("V", [P, 3, CB, H, VW])
        maxima = sb("maxima", [P, CB, H])
        maxT = sb("maxT", [H, CT], F32R)
        PT = sb("PT", [P, 4, CT])
        AOs = sb("AOs", [P, 2, CT])
        rden = sb("rden", [P, 2, 2, GH])
        att = sb("att", [P, CB, D])
        attT = sb("attT", [P, CT])
        yT_sb = sb("yT_sb", [P, CT])
        hT = sb("hT", [P, FF, CT])

        ps_max = ctx.enter_context(nc.psum_tensor("ps_max", [P, 2, CT], F32))
        ps_sc = ctx.enter_context(nc.psum_tensor("ps_sc", [P, 2, CT], F32))
        ps_ao = ctx.enter_context(nc.psum_tensor("ps_ao", [P, CT], F32))
        ps_misc = ctx.enter_context(nc.psum_tensor("ps_misc", [P, BANKS, CT], F32))

        def w(name, j=0):
            at = WCOLS[name][0] - W_FIRST + j * D
            return W[:, at:at + D]

        first = hT[:, :, :].rearrange("p j t -> p (j t)")[:, 0:W_FIRST]

        def w_first(name, j):
            return first[:, WCOLS[name][0] + j * D:WCOLS[name][0] + (j + 1) * D]

        def bcol(name):
            return bias[:, BIAS[name]:BIAS[name] + 1]

        def const(name):
            at, n = CONST[name]
            return cst[:, at:at + n]

        ident = const("ident")
        condT = first[:, WCOLS["condT"][0]:WCOLS["condT"][0] + B]

        names = ["rows_in", "x_in", "ctx_in", "small_in", "weights_in", "rest_in", "stored", "dve_chain",
                 "fixed_ready", "sums_zeroed", "exp_done", "silu_done", "mod_products", "vec_ready",
                 "var_ready", "vareps_ready", "rstd_ready", "xn_ready", "cn_ready", "xnT_ready", "cnT_ready", "misc_filled",
                 "rope_read", "rope_sums", "q_high", "q_low", "k_high", "k_low", "v_ready", "kd_in0", "kd_in1", "kd_in2", "kd_in3", "zeros_ready",
                 "max_scores", "max_taken", "maxT_ready", "q_stored", "k_stored", "max_stored",
                 "keys_in0", "keys_in1", "queries_in0", "queries_in1", "queries_in2", "maxima_in0", "maxima_in1", "maxima_in2",
                 "scores_ready", "probs_ready", "values_done", "sums_copied", "x_biased", "rden_ready",
                 "att_ready", "attT_ready", "hT_ready", "y_ready", "x_ready"]
        S = {n: sem(n) for n in names}
        GROUPS = NG * CB

        def bank(n):
            return ps_misc[:, n % BANKS, :]

        sources = {(st.kind, st.f): st.use for st in plan if st.kind in ("k", "q")}
        for st in plan:
            if st.kind in ("khi", "klo", "qhi", "qlo"):
                st.source = sources[st.kind[0], st.f]
        norm_use = [st.use for st in plan if st.kind == "norm"]
        biased = 0
        for st in plan:
            biased += st.kind == "bias"
            st.biased = biased
        mT_use = [st.use for st in plan if st.kind == "mT"]

        def f32(tile):
            return tile.bitcast(F32)

        def ns_of(st):
            return NS_CTX if ATTN[st.a]["cross"] else P

        feeds = {}
        update = {s: 0 for s in range(STREAMS)}
        normed = {s: 0 for s in range(STREAMS)}
        norms = [st for st in plan if st.kind in ("stats", "cstats")]
        for number, st in enumerate(norms):
            st.norm_no = number
        numbers = {(st.kind[-5:] == "stats" and st.kind[0] == "c", st.f, st.m): st.norm_no for st in norms}
        for st in plan:
            if st.kind in ("ln", "cln"):
                st.norm_no = numbers[st.kind == "cln", st.f, st.m]
        for st in plan:
            if st.kind == "ln" and st.m is None:
                feeds[st.f] = st.k
            if st.kind == "ln" and st.m is not None:
                feeds["mlp", st.m] = st.k
            if st.kind in ("stats", "store"):
                st.after = update[st.s]
            if st.kind in ("yT", "out"):
                update[st.s] = st.update
                st.norms_before = normed[st.s]
            if st.kind == "bias":
                st.norms_before = normed[st.s]
            if st.kind == "ln":
                normed[st.s] = st.k + 1

        xT_use = {st.k: st.use for st in plan if st.kind == "xT"}
        v_after_cT = {st.s: st.f + 1 for st in plan if st.kind == "v" and st.a == 1}

        def key_source(st):
            if not ATTN[st.a]["cross"]:
                return xnT[:, feeds[st.f] % 2, :]
            return cnT[:, :] if st.a == 1 else crawT[:, st.s, :]

        with nc.Block() as block:
            @block.sync
            def _(sp):
                def load_x(s):
                    sp.dma_start(x[:, s, :, :].rearrange("p b f -> p (b f)"),
                                 x_in[:, s * CB * D:(s + 1) * CB * D]).then_inc(S["x_in"], 16)

                load_x(0)
                sp.dma_start(first, weights[:, 0:W_FIRST]).then_inc(S["small_in"], 16)
                sp.dma_start(W[:, 0:W_SECOND - W_FIRST], weights[:, W_FIRST:W_SECOND]).then_inc(S["weights_in"], 16)
                sp.wait_ge(S["x_in"], 16)
                for s in range(1, STREAMS):
                    load_x(s)
                    sp.wait_ge(S["x_in"], 16 * (s + 1))
                sp.dma_start(craw[0:NS_CTX, :, :, :].rearrange("p s b f -> p (s b f)"),
                             ctx_in).then_inc(S["ctx_in"], 16)
                sp.wait_ge(S["ctx_in"], 16)
                sp.dma_start(crawT[:, :, :].rearrange("p s t -> p (s t)"), ctxT_in).then_inc(S["ctx_in"], 16)
                sp.dma_start(W[:, W_SECOND - W_FIRST:W_TOTAL - W_FIRST],
                             weights[:, W_SECOND:W_TOTAL]).then_inc(S["rest_in"], 16)
                sp.dma_start(bias_rows[:, :, :].rearrange("p a f -> p (a f)"), rows_in).then_inc(S["rows_in"], 16)
                for st in plan:
                    if st.kind == "kstore":
                        sp.wait_ge(S["k_high"], st.f + 1)
                        sp.dma_start(k_mem[st.f, :, 0:3:2, :], f32(Kh[:, st.f % 2, :])[:, None, :].to_broadcast(
                            [P, 2, CT])).then_inc(S["k_stored"], 16)
                        sp.wait_ge(S["k_low"], st.f + 1)
                        sp.dma_start(k_mem[st.f, :, 1, :], f32(Kl[:, :])).then_inc(S["k_stored"], 16)
                    elif st.kind == "qstore":
                        sp.wait_ge(S["q_high"], st.f + 1)
                        sp.dma_start(q_mem[st.f, :, 0:2, :], f32(Qh[:, st.f % 2, :])[:, None, :].to_broadcast(
                            [P, 2, CT])).then_inc(S["q_stored"], 16)
                        sp.wait_ge(S["q_low"], st.f + 1)
                        sp.dma_start(q_mem[st.f, :, 2, :], f32(Ql[:, :])).then_inc(S["q_stored"], 16)
                    elif st.kind == "kmask":
                        n, r = CB * ns_of(st), slice(HD * st.h, HD * st.h + HD)
                        if st.h == 0:
                            sp.wait_ge(S["k_high"], st.f + 1)
                        if st.h % HG == 0:
                            if st.f:
                                sp.wait_ge(S["max_scores"], CB * (NG * (st.f - 1) + st.h // HG + 1))
                            elif st.h == 0:
                                sp.wait_ge(S["zeros_ready"], 1)
                        sp.dma_start(f32(Kd[r, st.h, 0:n]),
                                     f32(Kh[r, st.f % 2, 0:n])).then_inc(S[f"kd_in{st.h // HG}"], 16)
                    elif st.kind == "kload":
                        n = CB * ns_of(st)
                        sp.wait_ge(S["k_stored"], 32 * (st.f + 1))
                        if st.f >= 2:
                            sp.wait_ge(S["scores_ready"], GROUPS * (st.f - 1))
                        sp.dma_start(f32(Ks[0:SROWS, st.f % 2, :, 0:n]),
                                     k_mem[st.f].rearrange("(n r) s t -> (r s) n t", n=NG)[:, :, 0:n]
                                     ).then_inc(S[f"keys_in{st.f % 2}"], 16)
                    elif st.kind == "qload":
                        half = 2 * st.f + st.g
                        sp.wait_ge(S["q_stored"], 32 * (st.f + 1))
                        if half >= 3:
                            sp.wait_ge(S["scores_ready"], GROUPS // 2 * (half - 2))
                        else:
                            sp.wait_ge(S["fixed_ready"], (3, 5, 6)[half])
                        heads = q_mem[st.f].rearrange("(n c r) s t -> c (r s) n t", n=NG, c=HG)
                        for c in range(HG):
                            sp.dma_start(f32(Qd[SR * c:SR * c + SR, half % 3, :, c, :]),
                                         heads[c][:, GP * st.g:GP * st.g + GP, :]
                                         ).then_inc(S[f"queries_in{half % 3}"], 16)
                    elif st.kind == "mstore":
                        sp.wait_ge(S["maxT_ready"], st.f + 1)
                        sp.dma_start(m_mem[st.f], f32(maxT[:, :])).then_inc(S["max_stored"], 16)
                    elif st.kind == "mload":
                        half = 2 * st.f + st.g
                        sp.wait_ge(S["max_stored"], 16 * (st.f + 1))
                        if half >= 3:
                            sp.wait_ge(S["scores_ready"], GROUPS // 2 * (half - 2))
                        sp.dma_start(f32(Qd[SROWS:SROWS + 1, half % 3, :, :, :]).rearrange("a n c t -> a (n c t)"),
                                     m_mem[st.f, GH * st.g:GH * st.g + GH, :].rearrange("(a h) t -> a (h t)", a=1)
                                     ).then_inc(S[f"maxima_in{half % 3}"], 16)
                    elif st.kind == "store":
                        sp.wait_ge(S["x_ready"], st.after)
                        sp.dma_start(out[:, st.s * CB * D:(st.s + 1) * CB * D],
                                     x[:, st.s, :, :].rearrange("p b f -> p (b f)")).then_inc(S["stored"], 16)
                sp.wait_ge(S["stored"], 16 * STREAMS)

            @block.vector
            def _(dve):
                chain = [0]

                def link(ins):
                    chain[0] += 1
                    return ins.then_inc(S["dve_chain"], 1)

                def linked():
                    dve.wait_ge(S["dve_chain"], chain[0])

                def statistics(src, rows, which):
                    for b in range(CB):
                        link(dve.bn_stats(stats[0:rows, which, b, :], src[0:rows, b, :]))
                    linked()
                    for b in range(CB):
                        dve.bn_aggr(mv[0:rows, which, b, :],
                                    stats[0:rows, which, b, :]).then_inc(S["var_ready"], 1)

                def norm(src, rows, dst, which, rstd_no, ready):
                    dve.wait_ge(S["rstd_ready"], rstd_no)
                    for b in range(CB):
                        dve.tensor_scalar(dst[0:rows, b, :], src[0:rows, b, :], mv[0:rows, which, b, 0:1],
                                          rstd[0:rows, which, b:b + 1], ALU.subtract,
                                          ALU.mult).then_inc(ready, 1)

                def rope(st):
                    ns, sums = (ns_of(st), 2 * rope_no(st.f)) if st.kind == "k" else (P, 2 * rope_no(st.f) + 1)
                    n = CB * ns
                    dve.wait_ge(S["k_low" if st.kind == "k" else "q_low"], st.f)
                    if sums:
                        dve.wait_ge(S["rope_sums"], sums)
                    total = ropeA[:, sums % 2, :]
                    for i, dst, table in ((0, total, "cos"), (1, ropeB, "sin")):
                        dve.wait_ge(S["misc_filled"], st.use + i + 1)
                        dve.tensor_tensor(dst[:, 0:n].rearrange("p (b t) -> p b t", b=CB),
                                          bank(st.use + i)[:, 0:n].rearrange("p (b t) -> p b t", b=CB),
                                          const(table)[:, None, 0:ns].to_broadcast([P, CB, ns]),
                                          ALU.mult).then_inc(S["rope_read"], 1)
                    dve.wait_ge(S["rope_read"], 2 * (sums + 1))
                    dve.tensor_tensor(total[:, 0:n], total[:, 0:n], ropeB[:, 0:n],
                                      ALU.add).then_inc(S["rope_sums"], 1)

                def low(st, high, dst, ready, stored, name, n):
                    if st.f:
                        dve.wait_ge(S[stored], 32 * st.f)
                    if ATTN[st.a]["rope"]:
                        ins = dve.tensor_tensor(dst[:, 0:n], ropeA[:, int(st.kind[0] == "q"), 0:n], high[:, 0:n], ALU.subtract)
                    else:
                        ins = dve.scalar_tensor_tensor(dst[:, 0:n], bank(st.source)[:, 0:n], bcol(name),
                                                       high[:, 0:n], ALU.add, ALU.subtract)
                    ins.then_inc(S[ready], 1)

                def modulation():
                    dve.wait_ge(S["mod_products"], 1)
                    for v in range(NV):
                        name = f"mod{v}" if v < 6 else f"ln{v - 6}"
                        one = 1.0 if v in (MULT_A, MULT_M, MULT_1, MULT_2, MULT_3) else 0.0
                        dve.tensor_scalar(vec[:, :, v], ps_sc[:, 0, v * B:(v + 1) * B], bcol(name), one,
                                          ALU.add, ALU.add).then_inc(S["vec_ready"], 1)

                dve.memset(ps_ao[:, :], 0.0).then_inc(S["sums_zeroed"], 1)
                dve.memset(f32(Kd[:, :, :]), 0.0).then_inc(S["zeros_ready"], 1)
                dve.wait_ge(S["exp_done"], 1)
                link(dve.tensor_scalar(silu[:, 1, :], silu[:, 0, :], 1.0, None, ALU.add))
                linked()
                link(dve.reciprocal(silu[:, 0, :], silu[:, 1, :]))
                linked()
                dve.tensor_tensor(silu[:, 2, :], condT, silu[:, 0, :], ALU.mult).then_inc(S["silu_done"], 1)
                for st in plan:
                    if st.kind == "stats":
                        if st.after:
                            dve.wait_ge(S["x_ready"], st.after)
                        else:
                            dve.wait_ge(S["x_in"], 16 * (st.s + 1))
                        statistics(x[:, st.s, :, :], P, 0)
                    elif st.kind == "cstats":
                        dve.wait_ge(S["ctx_in"], 16)
                        statistics(craw[:, st.s, :, :], NS_CTX, 1)
                    elif st.kind == "ln":
                        if st.k:
                            dve.wait_ge(S["misc_filled"], xT_use[st.k - 1] + 1)
                        norm(x[:, st.s, :, :], P, xn, 0, st.norm_no + 1, S["xn_ready"])
                        if st.k == 0:
                            modulation()
                    elif st.kind == "cln":
                        if st.k:
                            dve.wait_ge(S["cnT_ready"], st.k)
                        norm(craw[:, st.s, :, :], NS_CTX, cn, 1, st.norm_no + 1, S["cn_ready"])
                    elif st.kind in ("k", "q") and ATTN[st.a]["rope"]:
                        rope(st)
                    elif st.kind == "klo":
                        dve.wait_ge(S["k_high"], st.f + 1)
                        low(st, Kh[:, st.f % 2, :], Kl, "k_low", "k_stored", f"k{st.a}", CB * ns_of(st))
                    elif st.kind == "qlo":
                        dve.wait_ge(S["q_high"], st.f + 1)
                        low(st, Qh[:, st.f % 2, :], Ql, "q_low", "q_stored", f"q{st.a}", CT)
                    elif st.kind == "max":
                        ns = ns_of(st)
                        dve.wait_ge(S["max_scores"], st.k + 1)
                        dst = maxima[:, st.b, HG * st.n:HG * st.n + HG]
                        if st.n == 0 and st.b == 0 and st.f:
                            dve.wait_ge(S["misc_filled"], mT_use[st.f - 1] + 1)
                        dve.tensor_reduce(dst, ps_max[:, st.k % 2, 0:HG * ns].rearrange(
                            "p (h k) -> p h k", h=HG), AX_X, ALU.max, negate=True).then_inc(S["max_taken"], 1)
                    elif st.kind == "norm":
                        turned = bank(st.use).rearrange("p (b n c r) -> p b (n c) r", b=2, n=GP, c=HG)
                        dve.wait_ge(S["misc_filled"], st.use + 1)
                        dve.reciprocal(rden[:, st.k % 2, :, :], turned[:, :, :, HD]).then_inc(S["rden_ready"], 1)
                        dve.wait_ge(S["rden_ready"], st.k + 1)
                        if st.b == 0 and st.g == 0 and st.f:
                            dve.wait_ge(S["attT_ready"], st.f)
                        for i in range(2):
                            dve.tensor_tensor(att[:, st.b + i, GH * HD * st.g:GH * HD * (st.g + 1)].rearrange(
                                "p (h d) -> p h d", h=GH), turned[:, i, :, 0:HD],
                                rden[:, st.k % 2, i, :][:, :, None].to_broadcast([P, GH, HD]),
                                ALU.mult).then_inc(S["att_ready"], 1)
                    elif st.kind in ("o", "h2"):
                        if st.kind == "o":
                            gate = ATTN[st.a]["gate"]
                            add = bcol(f"o{st.a}") if ATTN[st.a]["bias"] else None
                        else:
                            gate, add = MLP[st.a]["gate"], bcol(f"b2_{st.a}")
                        dve.wait_ge(S["misc_filled"], st.use + 1)
                        src = bank(st.use)
                        if gate is not None:
                            for b in range(CB):
                                c = st.s * CB + b
                                ins = dve.tensor_scalar(yT_sb[:, b * P:(b + 1) * P], src[:, b * P:(b + 1) * P],
                                                        add, vec[:, c, gate:gate + 1], ALU.add, ALU.mult)
                        elif add is not None:
                            ins = dve.tensor_scalar(yT_sb[:, :], src, add, None, ALU.add)
                        else:
                            ins = dve.tensor_copy(yT_sb[:, :], src)
                        ins.then_inc(S["y_ready"], 1)
                    elif st.kind in ("yT", "out"):
                        dve.wait_ge(S["misc_filled"], st.use + 1)
                        dve.wait_ge(S["xn_ready"], CB * st.norms_before)
                        if st.biased:
                            dve.wait_ge(S["x_biased"], st.biased)
                        flat = x[:, st.s, :, :].rearrange("p b f -> p (b f)")
                        dve.tensor_tensor(flat, bank(st.use), flat, ALU.add).then_inc(S["x_ready"], 1)

            @block.gpsimd
            def _(pool):
                for number, (tile, value) in enumerate((
                        (minus_half[:, :], -0.5), (V[:, :, :, :, :], 1.0),
                        (f32(Qd[0:SROWS, 0, :, :, :]), 0.0), (f32(Ks[SROWS:SROWS + 1, :, :, :]), 1.0),
                        (f32(Qd[0:SROWS, 1, :, :, :]), 0.0), (f32(Qd[0:SROWS, 2, :, :, :]), 0.0))):
                    if number:
                        pool.wait_ge(S["fixed_ready"], number)
                    pool.memset(tile, value).then_inc(S["fixed_ready"], 1)
                for st in plan:
                    if st.kind in ("stats", "cstats"):
                        rows, which, eps = (P, 0, st.spec["eps"]) if st.kind == "stats" else (NS_CTX, 1, 1e-6)
                        pool.wait_ge(S["var_ready"], CB * (st.norm_no + 1))
                        pool.tensor_scalar(vareps[0:rows, which, :], mv[0:rows, which, :, 1], eps, None,
                                           ALU.add).then_inc(S["vareps_ready"], 1)
                        pool.wait_ge(S["vareps_ready"], st.norm_no + 1)
                        pool.tensor_tensor(rstd[0:rows, which, :], vareps[0:rows, which, :],
                                           minus_half[0:rows, :], ALU.pow).then_inc(S["rstd_ready"], 1)
                    elif st.kind == "bias":
                        pool.wait_ge(S["xn_ready"], CB * st.norms_before)
                        which = 0 if st.m is None else 1
                        if st.k == 0:
                            pool.wait_ge(S["rows_in"], 16)
                        pool.tensor_tensor(x[:, st.s, :, :], x[:, st.s, :, :],
                                           bias_rows[:, which, :][:, None, :].to_broadcast([P, CB, D]),
                                           ALU.add).then_inc(S["x_biased"], 1)

            @block.scalar
            def _(act):
                act.dma_start(bias[:, :], biases).then_inc(S["small_in"], 16)
                act.dma_start(cst[:, :], consts).then_inc(S["small_in"], 16)
                act.wait_ge(S["small_in"], 48)
                act.activation(silu[:, 0, :], condT, ACT.Exp, scale=-1.0).then_inc(S["exp_done"], 1)
                for st in plan:
                    if st.kind == "cT":
                        act.wait_ge(S["misc_filled"], st.use + 1)
                        if st.k:
                            act.wait_ge(S["v_ready"], v_after_cT[st.k - 1])
                        act.activation(cnT[:, :], bank(st.use)[:, 0:CB * NS_CTX],
                                       ACT.Copy).then_inc(S["cnT_ready"], 1)
                    elif st.kind in ("khi", "qhi"):
                        k = st.kind == "khi"
                        n = CB * ns_of(st) if k else CT
                        high = (Kh if k else Qh)[:, st.f % 2, 0:n]
                        if st.f >= 2:
                            if k:
                                act.wait_ge(S["k_stored"], 32 * (st.f - 1))
                                act.wait_ge(S["max_scores"], GROUPS * (st.f - 1))
                            else:
                                act.wait_ge(S["q_stored"], 32 * (st.f - 1))
                                act.wait_ge(S["max_scores"], GROUPS * (st.f - 1))
                        if ATTN[st.a]["rope"]:
                            act.wait_ge(S["rope_sums"], 2 * rope_no(st.f) + (1 if k else 2))
                            ins = act.activation(high, ropeA[:, int(not k), 0:n], ACT.Copy)
                        else:
                            act.wait_ge(S["misc_filled"], st.source + 1)
                            ins = act.activation(high, bank(st.source)[:, 0:n], ACT.Identity,
                                                 bias=bcol(f"k{st.a}" if k else f"q{st.a}"))
                        ins.then_inc(S["k_high" if k else "q_high"], 1)
                    elif st.kind == "v":
                        ns = ns_of(st)
                        act.wait_ge(S["misc_filled"], st.use + 1)
                        if st.f >= 3:
                            act.wait_ge(S["values_done"], GROUPS * (st.f - 2))
                        elif st.f == 0:
                            act.wait_ge(S["fixed_ready"], 2)
                        act.activation(V[0:ns, st.f % 3, :, :, 0:HD],
                                       bank(st.use)[0:ns, :].rearrange("p (b h d) -> p b h d", b=CB, h=H),
                                       ACT.Copy).then_inc(S["v_ready"], 1)
                    elif st.kind == "xT":
                        act.wait_ge(S["misc_filled"], st.use + 1)
                        if st.k == 0:
                            act.wait_ge(S["vec_ready"], NV)
                        src, dst = bank(st.use), xnT[:, st.k % 2, :]
                        if st.spec["mult"] is None:
                            act.activation(dst, src, ACT.Copy).then_inc(S["xnT_ready"], CB)
                        else:
                            for b in range(CB):
                                c, m, sh = st.s * CB + b, st.spec["mult"], st.spec["shift"]
                                act.activation(dst[:, b * P:(b + 1) * P], src[:, b * P:(b + 1) * P], ACT.Identity,
                                               scale=vec[:, c, m:m + 1],
                                               bias=vec[:, c, sh:sh + 1]).then_inc(S["xnT_ready"], 1)
                    elif st.kind == "mT":
                        act.wait_ge(S["misc_filled"], st.use + 1)
                        if st.f:
                            act.wait_ge(S["max_stored"], 16 * st.f)
                        act.activation(maxT[:, :], bank(st.use)[0:H, :], ACT.Copy).then_inc(S["maxT_ready"], 1)
                    elif st.kind == "score":
                        ns = ns_of(st)
                        act.wait_ge(S["scores_ready"], st.k + 1)
                        if st.k >= 4:
                            act.wait_ge(S["values_done"], st.k - 3)
                        act.activation(PT[0:ns, st.k % 4, :], ps_sc[0:ns, st.k % 2, :], ACT.Exp,
                                       scale=SCALE).then_inc(S["probs_ready"], 1)
                    elif st.kind == "copy":
                        act.wait_ge(S["values_done"], HG * (st.k + 1))
                        if st.k >= 2:
                            act.wait_ge(S["misc_filled"], norm_use[st.k - 2] + 1)
                        act.activation(AOs[:, st.k % 2, :], ps_ao[:, :], ACT.Copy).then_inc(S["sums_copied"], 1)
                    elif st.kind == "aT":
                        act.wait_ge(S["misc_filled"], st.use + 1)
                        if ATTN[st.a]["bias"]:
                            ins = act.activation(attT[:, :], bank(st.use), ACT.Identity, bias=bcol(f"v{st.a}"))
                        else:
                            ins = act.activation(attT[:, :], bank(st.use), ACT.Copy)
                        ins.then_inc(S["attT_ready"], 1)
                    elif st.kind == "h":
                        act.wait_ge(S["misc_filled"], st.use + 1)
                        act.activation(hT[:, st.j, :], bank(st.use),
                                       ACT.Gelu_apprx_tanh if MLP[st.a]["act"] == "tanh" else ACT.Gelu,
                                       bias=bcol(f"b1_{st.a}_{st.j}")).then_inc(S["hT_ready"], 1)

            @block.tensor
            def _(pe):
                def fill(n):
                    if n >= BANKS:
                        pe.wait_ge(S[uses[n - BANKS][0]], uses[n - BANKS][1])

                def turn(src, use, rows=P):
                    for b in range(CB):
                        last = pe.transpose(bank(use)[:, b * rows:(b + 1) * rows], src[0:rows, b, :],
                                            ident[0:rows, 0:rows])
                    last.then_inc(S["misc_filled"], 1)

                pe.wait_ge(S["silu_done"], 1)
                for v in range(NV):
                    lhs, rhs = ((w_first("mod", v), silu[:, 2, :]) if v < 6 else
                                (w_first("ln", v - 6), condT))
                    last = pe.matmul(ps_sc[:, 0, v * B:(v + 1) * B], lhs, rhs, start=True, stop=True)
                last.then_inc(S["mod_products"], 1)
                for st in plan:
                    if st.kind == "xT":
                        fill(st.use)
                        pe.wait_ge(S["xn_ready"], CB * (st.k + 1))
                        turn(xn, st.use)
                    elif st.kind == "cT":
                        fill(st.use)
                        pe.wait_ge(S["cn_ready"], CB * (st.k + 1))
                        turn(cn, st.use, NS_CTX)
                    elif st.kind in ("k", "q"):
                        n = CB * (ns_of(st) if st.kind == "k" else P)
                        if st.kind == "k":
                            if st.a == 0 or st.a == 2:
                                pe.wait_ge(S["xnT_ready"], CB * (feeds[st.f] + 1))
                            elif st.a == 1:
                                pe.wait_ge(S["cnT_ready"], st.s + 1)
                            else:
                                pe.wait_ge(S["ctx_in"], 32)
                            if st.f == 0:
                                pe.wait_ge(S["weights_in"], 16)
                            src = key_source(st)
                        else:
                            pe.wait_ge(S["xnT_ready"], CB * (feeds[st.f] + 1))
                            src = xnT[:, feeds[st.f] % 2, :]
                        forms = ["", "s"] if ATTN[st.a]["rope"] else [""]
                        for i, form in enumerate(forms):
                            fill(st.use + i)
                            pe.matmul(bank(st.use + i)[:, 0:n], w(f"{st.kind}{st.a}{form}"), src[:, 0:n],
                                      start=True, stop=True).then_inc(S["misc_filled"], 1)
                    elif st.kind == "v":
                        ns = ns_of(st)
                        fill(st.use)
                        src = key_source(st)
                        for b in range(CB):
                            last = pe.matmul(bank(st.use)[0:ns, b * D:(b + 1) * D], src[:, b * ns:(b + 1) * ns],
                                             w(f"v{st.a}"), start=True, stop=True)
                        last.then_inc(S["misc_filled"], 1)
                    elif st.kind == "max":
                        ns = ns_of(st)
                        if st.b == 0:
                            pe.wait_ge(S[f"kd_in{st.n}"], 16 * HG * (st.f + 1))
                        if st.b == 0 and st.n == 0:
                            pe.wait_ge(S["q_high"], st.f + 1)
                        if st.k >= 2:
                            pe.wait_ge(S["max_taken"], st.k - 1)
                        pe.matmul(ps_max[:, st.k % 2, 0:HG * ns], Qh[:, st.f % 2, st.b * P:(st.b + 1) * P],
                                  Kd[:, HG * st.n:HG * st.n + HG, st.b * ns:(st.b + 1) * ns],
                                  start=True, stop=True).then_inc(S["max_scores"], 1)
                    elif st.kind == "mT":
                        fill(st.use)
                        pe.wait_ge(S["max_taken"], GROUPS * (st.f + 1))
                        for b in range(CB):
                            last = pe.transpose(bank(st.use)[0:H, b * P:(b + 1) * P], maxima[:, b, :], ident)
                        last.then_inc(S["misc_filled"], 1)
                    elif st.kind == "score":
                        ns, half = ns_of(st), 2 * st.f + st.n // GP
                        if st.b == 0 and st.n % GP == 0:
                            pe.wait_ge(S[f"queries_in{half % 3}"], 16 * HG * (half // 3 + 1))
                            pe.wait_ge(S[f"maxima_in{half % 3}"], 16 * (half // 3 + 1))
                        if st.b == 0 and st.n == 0:
                            pe.wait_ge(S[f"keys_in{st.f % 2}"], 16 * (st.f // 2 + 1))
                            if st.f == 0:
                                pe.wait_ge(S["fixed_ready"], 4)
                        if st.k >= 2:
                            pe.wait_ge(S["probs_ready"], st.k - 1)
                        pe.matmul(ps_sc[0:ns, st.k % 2, :], Ks[:, st.f % 2, st.n, st.b * ns:(st.b + 1) * ns],
                                  Qd[:, half % 3, st.n % GP, :, st.b * P:(st.b + 1) * P],
                                  start=True, stop=True).then_inc(S["scores_ready"], 1)
                    elif st.kind == "value":
                        ns = ns_of(st)
                        pe.wait_ge(S["probs_ready"], st.k + 1)
                        if st.b == 0 and st.n == 0:
                            pe.wait_ge(S["v_ready"], st.f + 1)
                        if st.k % NG == 0 and st.k:
                            pe.wait_ge(S["sums_copied"], st.k // NG)
                        at = (st.b % 2 * GP + st.n % GP) * P
                        for c in range(HG):
                            last = pe.matmul(ps_ao[32 * c:32 * c + VW, at:at + P],
                                             V[0:ns, st.f % 3, st.b, HG * st.n + c, :],
                                             PT[0:ns, st.k % 4, c * P:(c + 1) * P], start=True, stop=True)
                        last.then_inc(S["values_done"], 1)
                    elif st.kind == "norm":
                        fill(st.use)
                        pe.wait_ge(S["sums_copied"], st.k + 1)
                        for n in range(NG):
                            last = pe.transpose(bank(st.use)[:, n * P:(n + 1) * P], AOs[:, st.k % 2, n * P:(n + 1) * P],
                                                ident)
                        last.then_inc(S["misc_filled"], 1)
                    elif st.kind == "aT":
                        fill(st.use)
                        pe.wait_ge(S["att_ready"], 2 * CB * (st.f + 1))
                        turn(att, st.use)
                    elif st.kind == "o":
                        fill(st.use)
                        pe.wait_ge(S["attT_ready"], st.f + 1)
                        pe.matmul(bank(st.use), w(f"o{st.a}"), attT[:, :], start=True,
                                  stop=True).then_inc(S["misc_filled"], 1)
                    elif st.kind == "h":
                        fill(st.use)
                        pe.wait_ge(S["xnT_ready"], CB * (feeds["mlp", st.m] + 1))
                        if st.k == 0:
                            pe.wait_ge(S["rest_in"], 16)
                        pe.matmul(bank(st.use), w(f"w1_{st.a}", st.j), xnT[:, feeds["mlp", st.m] % 2, :],
                                  start=True, stop=True).then_inc(S["misc_filled"], 1)
                    elif st.kind == "h2":
                        fill(st.use)
                        pe.wait_ge(S["hT_ready"], FF * (st.m + 1))
                        for j in range(FF):
                            last = pe.matmul(bank(st.use), w(f"w2_{st.a}", j), hT[:, j, :], start=(j == 0),
                                             stop=(j == FF - 1))
                        last.then_inc(S["misc_filled"], 1)
                    elif st.kind == "out":
                        fill(st.use)
                        if st.m is None:
                            pe.wait_ge(S["attT_ready"], st.f + 1)
                            parts = [(attT[:, :], w(f"o{st.a}"))]
                        else:
                            pe.wait_ge(S["hT_ready"], FF * (st.m + 1))
                            parts = [(hT[:, j, :], w(f"w2_{st.a}", j)) for j in range(FF)]
                        for b in range(CB):
                            for i, (src, weight) in enumerate(parts):
                                last = pe.matmul(bank(st.use)[:, b * D:(b + 1) * D], src[:, b * P:(b + 1) * P],
                                                 weight, start=(i == 0), stop=(i == len(parts) - 1))
                        last.then_inc(S["misc_filled"], 1)
                    elif st.kind == "yT":
                        fill(st.use)
                        pe.wait_ge(S["y_ready"], st.k + 1)
                        for b in range(CB):
                            last = pe.transpose(bank(st.use)[:, b * P:(b + 1) * P], yT_sb[:, b * P:(b + 1) * P],
                                                ident)
                        last.then_inc(S["misc_filled"], 1)


def _constants():
    c = np.zeros((P, NCONST), np.float32)
    p = np.arange(P)
    at = CONST["ident"][0]
    c[p, at + p] = 1.0
    half = HD // 2
    inv = (1.0 / np.float32(10000.0) ** (np.arange(half, dtype=np.float32) / half)).astype(np.float32)
    ang = (np.arange(P, dtype=np.float32)[None, :] * inv[p % half][:, None]).astype(np.float32)
    at = CONST["cos"][0]
    c[:, at:at + P] = np.cos(ang)
    at = CONST["sin"][0]
    c[:, at:at + P] = np.sin(ang) * np.where(p % HD < half, -1.0, 1.0)[:, None].astype(np.float32)
    return c


def kernel(**inputs):
    import concourse.bacc as _bacc
    from concourse.bass_utils import run_bass_kernel_spmd as _run

    i = {n: np.asarray(a) for n, a in inputs.items()}
    L0, L1 = "L0_xcond_", "L1_xcond_"

    def blocks(a):
        return a.reshape(-1, P, a.shape[1]).transpose(1, 0, 2).reshape(P, -1)

    swap = (np.arange(D) // HD) * HD + (np.arange(D) + HD // 2) % HD
    qkv0, kvc0 = i[L0 + "W_qkv"], i[L0 + "W_kvc"]
    qkv1 = i[L1 + "qkv_w"].T
    parts = {
        "mod": i[L0 + "W_mod"],
        "ln": np.concatenate([i[L1 + f"ln{n}_w"].T for n in (1, 2, 3)], axis=1),
        "condT": i["cond_1024"].T,
        "q0": qkv0[:, 0:D], "k0": qkv0[:, D:2 * D], "v0": qkv0[:, 2 * D:], "o0": i[L0 + "W_proj"],
        "q1": i[L0 + "W_qc"], "k1": kvc0[:, 0:D], "v1": kvc0[:, D:], "o1": i[L0 + "W_cproj"],
        "w1_0": i[L0 + "W_mlp1"], "w2_0": blocks(i[L0 + "W_mlp2"]),
        "q2": qkv1[:, 0:D], "q2s": qkv1[:, 0:D][:, swap], "k2": qkv1[:, D:2 * D],
        "k2s": qkv1[:, D:2 * D][:, swap], "v2": qkv1[:, 2 * D:], "o2": i[L1 + "sa_out_w"].T,
        "q3": i[L1 + "q_w"].T, "q3s": i[L1 + "q_w"].T[:, swap], "k3": i[L1 + "k_w"].T,
        "k3s": i[L1 + "k_w"].T[:, swap], "v3": i[L1 + "v_w"].T, "o3": i[L1 + "ca_out_w"].T,
        "w1_1": i[L1 + "ffn_w1"].T, "w2_1": blocks(i[L1 + "ffn_w2"].T),
    }
    weights = np.concatenate([parts[n] for n in WCOLS], axis=1)
    bq = i[L0 + "b_qkv"].reshape(3, D)
    bkv = i[L0 + "b_kvc"].reshape(2, D)
    biases = np.concatenate([
        i[L0 + "b_mod"].reshape(6, D), i[L1 + "ln1_b"].reshape(2, D), i[L1 + "ln2_b"].reshape(2, D),
        i[L1 + "ln3_b"].reshape(2, D), bq, i[L0 + "b_proj"][None], i[L0 + "b_qc"][None], bkv,
        i[L0 + "b_cproj"][None], i[L0 + "b_mlp1"].reshape(FF, D), i[L0 + "b_mlp2"][None],
        i[L1 + "ffn_b1"].reshape(FF, D), i[L1 + "ffn_b2"][None]], axis=0).T
    arrays = {
        "weights": weights, "biases": biases, "consts": _constants(),
        "x_in": i["x"].transpose(1, 0, 2).reshape(P, B * D),
        "ctx_in": i["ctx_1024"].transpose(1, 0, 2).reshape(NS_CTX, B * D),
        "ctxT_in": i["ctx_1024"].transpose(2, 0, 1).reshape(D, B * NS_CTX),
        "rows_in": np.broadcast_to(np.concatenate([i[L0 + "b_cproj"], i[L1 + "ffn_b2"]]), (P, 2 * D)),
    }
    arrays = {n: np.ascontiguousarray(a) for n, a in arrays.items()}
    nc = _bacc.Bacc("TRN2", target_bir_lowering=False, num_devices=1)
    args = [nc.dram_tensor(n, a.shape, F32, kind="ExternalInput").ap() for n, a in arrays.items()]
    out = nc.dram_tensor("out", (P, B * D), F32, kind="ExternalOutput").ap()
    units = len(ATTN) * STREAMS
    mem = [nc.dram_tensor(n, shape, F32, kind="Internal").ap() for n, shape in
           (("q_mem", (units, P, SPLIT, CT)), ("k_mem", (units, P, SPLIT, CT)), ("m_mem", (units, H, CT)))]
    block_kernel(nc, *args, *mem, out)
    r = _run(nc, [arrays], core_ids=[0])
    return np.ascontiguousarray(np.asarray(r.results[0]["out"]).reshape(P, B, D).transpose(1, 0, 2))
```

```python
from contextlib import ExitStack

import numpy as np

from concourse import mybir

ALU = mybir.AluOpType
ACT = mybir.ActivationFunctionType
AX_X = mybir.AxisListType.X
F32 = mybir.dt.float32
F32R = mybir.dt.float32r

P = 128
D = 128
B = 16
NS_CTX = 120
H = 16
HD = D // H
SCALE = HD ** -0.5
CB = 4
CT = CB * P
STREAMS = B // CB
HG = 4
NG = H // HG
GH = H // 2
GP = NG // 2
SPLIT = 3
SR = SPLIT * HD
SROWS = HG * SR
FF = 4
BANKS = 3
MAX_BANKS = 2
VW = HD + 1

WCOLS = {}


def _pack_names():
    names = [("mod", 6 * D), ("ln", 6 * D), ("condT", B),
             ("q0", D), ("k0", D), ("v0", D), ("o0", D),
             ("q1", D), ("k1", D), ("v1", D), ("o1", D), ("w1_0", FF * D), ("w2_0", FF * D),
             ("q2", D), ("q2s", D), ("k2", D), ("k2s", D), ("v2", D), ("o2", D),
             ("q3", D), ("q3s", D), ("k3", D), ("k3s", D), ("v3", D), ("o3", D),
             ("w1_1", FF * D), ("w2_1", FF * D)]
    at = 0
    for n, w in names:
        WCOLS[n] = (at, w)
        at += w
    return at


W_TOTAL = _pack_names()
W_FIRST = WCOLS["q0"][0]
W_SECOND = WCOLS["w1_0"][0]

BIAS = {n: i for i, n in enumerate(
    ["mod0", "mod1", "mod2", "mod3", "mod4", "mod5", "ln0", "ln1", "ln2", "ln3", "ln4", "ln5",
     "q0", "k0", "v0", "o0", "q1", "k1", "v1", "o1",
     "b1_0_0", "b1_0_1", "b1_0_2", "b1_0_3", "b2_0", "b1_1_0", "b1_1_1", "b1_1_2", "b1_1_3", "b2_1"])}
NB = len(BIAS)

CONST = {"ident": (0, P), "cos": (P, P), "sin": (2 * P, P)}
NCONST = 3 * P

SHIFT_A, MULT_A, GATE_A, SHIFT_M, MULT_M, GATE_M, MULT_1, SHIFT_1, MULT_2, SHIFT_2, MULT_3, SHIFT_3 = range(12)
NV = 12

ATTN = [
    dict(eps=1e-6, mult=MULT_A, shift=SHIFT_A, cross=False, rope=False, gate=GATE_A, bias=True),
    dict(eps=1e-6, mult=None, shift=None, cross=True, rope=False, gate=None, bias=True),
    dict(eps=1e-5, mult=MULT_1, shift=SHIFT_1, cross=False, rope=True, gate=None, bias=False),
    dict(eps=1e-5, mult=MULT_2, shift=SHIFT_2, cross=True, rope=True, gate=None, bias=False),
]
MLP = [
    dict(eps=1e-6, mult=MULT_M, shift=SHIFT_M, gate=GATE_M, act="tanh"),
    dict(eps=1e-5, mult=MULT_3, shift=SHIFT_3, gate=None, act="erf"),
]


class Step:

    def __init__(self, kind, a=None, s=None, f=None, m=None, b=None, n=None, h=None, g=None, j=None, spec=None):
        self.kind = kind
        self.a = a
        self.s = s
        self.f = f
        self.m = m
        self.b = b
        self.n = n
        self.h = h
        self.g = g
        self.j = j
        self.spec = spec
        self.k = 0
        self.use = 0


T = dict(
    hstep=(0.0, 0.1),
    hlate=(0.6, 0.4),
    ln=(-36.25, -33.4, -34.0, -35.0),
    xT=(-33.75, -30.6, -31.0, -31.0),
    k=(-30.6, -30.4, -29.75, -30.75),
    q=(-29.2, -29.2, -28.55, -29.05),
    v=(-24.95, -25.2, -25.3, -26.95),
    kmask=(-29.0, -29.4, -28.9, -30.4),
    kstep=(1.52, 1.62, 1.41, 1.44),
    max=(-25.8, -24.3, -24.3, -24.3),
    mstep=(1.05, 1.05, 1.05, 1.05),
    mT=(-8.9, -7.3, -7.3, -7.4),
    kload=(-15, -17, -13.1, -15.3),
    qload=(-15.1, -14.4, -15.2, -17.2),
    mload=(-9.4, -6.3, -6.4, -7.0),
    copy=(0.3, 0.3, 0.1, 0.3),
    norm=(4.0, 2.0, 3.0, 2.9),
    aT=(4.8, 3.8, 4.8, 4.55),
    o=(5.7, 4.7, 5.2, 5.55),
    yT=(8.9, 9.9, 6.9, 10.05),
    mln=(7.3, 7.55),
    mxT=(8.7, 9.35),
    mh=(9.4, 12.15),
    mh2=(11.0, 14.05),
    myT=(12.0, 11.45),
    bias=(-8.6, -12.0, -10.1, -11.7),
    apply=(1.7, 1.8, 1.8, 0.8),
    kstore=(1.1, 2.6, 0.6, 0.1),
    qstore=(0.5, 3.8, 0.8, -0.6),
    mstore=(-2.0, -1.0, -0.2, -2.8),
    msecond=(0.4, -0.3, 0.1, 2.1),
    qsecond=(9.4, 9.0, 13.3, 6.8),
    klo=(1.7, 1.3, 1.4, 3.45),
    qlo=(1.3, 1.3, 1.3, 0.95),
    khi=(0.35, 0.3, 1.0, 1.35),
    qhi=(0.35, 0.1, 1.3, 1.35),
    value=(1.1, 1.1, 1.1, 1.1),
    cln=(-36.45, -35.85, -38.4, -36.0),
    cT=(-36.95, -34.55, -37.3, -33.7),
    mapply=(2.0, 1.3),
)

EARLY = [-0.6, 0.4, 0.6, 0]
MLP_LATER = {6: 12.1}


def make_plan():
    steps = []

    def at(when, st, late=None):
        steps.append((when, len(steps), st))
        st.late = when if late is None else late, len(steps)

    cells = [(b, n) for g in range(2) for b in range(CB) for n in range(GP * g, GP * g + GP)]
    period = len(cells)
    for f in range(len(ATTN) * STREAMS):
        a, s, t = f // STREAMS, f % STREAMS, period * f
        who = dict(f=f, a=a, s=s)
        front = t - EARLY[min(f, len(EARLY) - 1)]
        if a == 1:
            at(front + T["cln"][a] - T["apply"][a], Step("cstats", **who))
            at(front + T["cln"][a], Step("cln", **who))
            at(front + T["cT"][a], Step("cT", **who))
        at(front + T["ln"][a] - T["apply"][a], Step("stats", spec=ATTN[a], **who))
        at(front + T["ln"][a], Step("ln", spec=ATTN[a], **who))
        at(front + T["xT"][a], Step("xT", spec=ATTN[a], **who))
        at(front + T["k"][a], Step("k", **who))
        at(front + T["q"][a], Step("q", **who))
        for x in "kq":
            at(front + T[x][a] + T[x + "hi"][a], Step(x + "hi", **who))
            at(front + T[x][a] + T[x + "lo"][a], Step(x + "lo", **who))
            at(front + T[x][a] + T[x + "lo"][a] + T[x + "store"][a], Step(x + "store", **who))
        at(front + T["v"][a], Step("v", **who))
        for h in range(H):
            at(t + T["kmask"][a] + h // HG * T["kstep"][a], Step("kmask", h=h, **who))
        for i in range(period):
            at(t + T["max"][a] + i * T["mstep"][a], Step("max", n=i // CB, b=i % CB, **who))
        at(t + T["mT"][a], Step("mT", **who))
        at(t + T["mT"][a] + T["mstore"][a], Step("mstore", **who))
        at(t + T["kload"][a], Step("kload", **who))
        for g in range(2):
            at(t + T["qload"][a] + T["qsecond"][a] * g, Step("qload", g=g, **who))
            at(t + T["mload"][a] + T["msecond"][a] * g, Step("mload", g=g, **who))
        for i, (b, n) in enumerate(cells):
            at(t + i, Step("score", b=b, n=n, **who))
            at(t + i + T["value"][a], Step("value", b=b, n=n, **who))
        for i in range(CB):
            bank = dict(g=i // 2, b=i % 2 * 2)
            at(t + NG * i + NG + T["copy"][a], Step("copy", **bank, **who))
            at(t + NG * i + NG + T["norm"][a], Step("norm", **bank, **who))
        at(t + period + T["aT"][a], Step("aT", **who))
        if ATTN[a]["gate"] is None:
            if ATTN[a]["bias"]:
                at(t + T["bias"][a], Step("bias", **who))
            at(t + period + T["o"][a], Step("out", **who))
        else:
            at(t + period + T["o"][a], Step("o", **who))
            at(t + period + T["yT"][a], Step("yT", **who))
        if a % 2:
            layer, t = a // 2, t + period
            who = dict(m=layer * STREAMS + s, a=layer, s=s)
            t += MLP_LATER.get(who["m"], 0)
            at(t + T["mln"][layer] - T["mapply"][layer], Step("stats", spec=MLP[layer], **who))
            at(t + T["mln"][layer], Step("ln", spec=MLP[layer], **who))
            at(t + T["mxT"][layer], Step("xT", spec=MLP[layer], **who))
            for j in range(FF):
                at(t + T["mh"][layer] + j * T["hstep"][layer], Step("h", j=j, **who),
                   late=t + T["mh"][layer] + T["hlate"][layer])
            if MLP[layer]["gate"] is None:
                at(t + T["mh"][layer] - 0.1, Step("bias", **who))
                at(t + T["mh2"][layer], Step("out", **who))
                at(t + T["mh2"][layer] + 0.1, Step("store", **who))
            else:
                at(t + T["mh2"][layer], Step("h2", **who))
                at(t + T["myT"][layer], Step("yT", **who))
    plan = [st for _, _, st in sorted(steps, key=lambda x: x[:2])]
    for s in range(STREAMS):
        done, unit = 0, None
        for st in plan:
            if st.s == s and st.kind == "stats":
                assert done == (st.a + st.a // 2 if st.m is None else 3 * st.a + 2), "a norm before its input"
            done += st.s == s and st.kind in ("yT", "out")
            if st.s == s and st.kind in ("ln", "bias", "yT", "out"):
                assert (st.a, st.m) == unit or st.kind == "ln", "a bias or an update before its norm"
                unit = (st.a, st.m)
    order = [st.kind for st in plan if st.kind in ("stats", "ln")]
    assert order == ["stats", "ln"] * (len(order) // 2), "statistics overwritten"
    order = [st.kind for st in plan if st.kind in ("cstats", "cln")]
    assert order == ["cstats", "cln"] * (len(order) // 2), "statistics overwritten"
    seen = {}
    for st in plan:
        st.k = seen.get(st.kind, 0)
        seen[st.kind] = st.k + 1
    uses, turned, updates = [], 0, 0
    for st in plan:
        st.use = len(uses)
        if st.kind == "xT":
            uses.append(("xnT_ready", CB * (st.k + 1)))
        elif st.kind == "cT":
            uses.append(("cnT_ready", st.k + 1))
        elif st.kind == "q":
            uses += ([("rope_read", 4 * rope_no(st.f) + 3), ("rope_read", 4 * rope_no(st.f) + 4)]
                     if ATTN[st.a]["rope"] else [("q_low", st.f + 1)])
        elif st.kind == "k":
            uses += ([("rope_read", 4 * rope_no(st.f) + 1), ("rope_read", 4 * rope_no(st.f) + 2)]
                     if ATTN[st.a]["rope"] else [("k_low", st.f + 1)])
        elif st.kind == "v":
            uses.append(("v_ready", st.k + 1))
        elif st.kind == "mT":
            uses.append(("maxT_ready", st.k + 1))
        elif st.kind == "aT":
            uses.append(("attT_ready", st.k + 1))
        elif st.kind == "h":
            uses.append(("hT_ready", st.k + 1))
        elif st.kind in ("o", "h2"):
            turned += 1
            uses.append(("y_ready", turned))
        elif st.kind == "norm":
            uses.append(("att_ready", 2 * (st.k + 1)))
        elif st.kind in ("yT", "out"):
            updates += 1
            st.update = updates
            uses.append(("x_ready", updates))
    return plan, sorted(plan, key=lambda st: st.late), uses


def rope_no(f):
    return sum(ATTN[g // STREAMS]["rope"] for g in range(f))


def block_kernel(nc, weights, biases, consts, x_in, ctx_in, ctxT_in, rows_in, q_mem, k_mem, m_mem, out):
    plan, late, uses = make_plan()

    with ExitStack() as ctx:
        def sb(name, shape, dt=F32):
            return ctx.enter_context(nc.sbuf_tensor(name, shape, dt))

        def sem(name):
            return ctx.enter_context(nc.semaphore(name))

        W = sb("W", [P, W_TOTAL - W_FIRST])
        bias = sb("bias", [P, NB])
        bias_rows = sb("bias_rows", [P, 2, D])
        cst = sb("cst", [P, NCONST])
        silu = sb("silu", [P, 3, B])
        vec = sb("vec", [P, B, NV])
        x = sb("x", [P, STREAMS, CB, D])
        craw = sb("craw", [P, STREAMS, CB, D])
        crawT = sb("crawT", [P, STREAMS, CB * NS_CTX])
        cnT = sb("cnT", [P, CB * NS_CTX])
        cn = sb("cn", [P, CB, D])
        stats = sb("stats", [P, 2, CB, 6])
        mv = sb("mv", [P, 2, CB, 2])
        vareps = sb("vareps", [P, 2, CB])
        rstd = sb("rstd", [P, 2, CB])
        minus_half = sb("minus_half", [P, CB])
        xn = sb("xn", [P, CB, D])
        xnT = sb("xnT", [P, 2, CT])
        ropeA = sb("ropeA", [P, 2, CT])
        ropeB = sb("ropeB", [P, CT])
        Qh = sb("Qh", [P, 2, CT], F32R)
        Ql = sb("Ql", [P, CT], F32R)
        Kh = sb("Kh", [P, 2, CT], F32R)
        Kl = sb("Kl", [P, CT], F32R)
        Kd = sb("Kd", [P, H, CT], F32R)
        Ks = sb("Ks", [SROWS + 1, 2, NG, CT], F32R)
        Qd = sb("Qd", [SROWS + 1, 3, GP, HG, CT], F32R)
        V = sb("V", [P, 3, CB, H, VW])
        maxima = sb("maxima", [P, CB, H])
        maxT = sb("maxT", [H, CT], F32R)
        PT = sb("PT", [P, 4, CT])
        AOs = sb("AOs", [P, 2, CT])
        rden = sb("rden", [P, 2, 2, GH])
        att = sb("att", [P, CB, D])
        attT = sb("attT", [P, CT])
        yT_sb = sb("yT_sb", [P, CT])
        hT = sb("hT", [P, FF, CT])

        ps_max = ctx.enter_context(nc.psum_tensor("ps_max", [P, MAX_BANKS, CT], F32))
        ps_sc = ctx.enter_context(nc.psum_tensor("ps_sc", [P, 2, CT], F32))
        ps_ao = ctx.enter_context(nc.psum_tensor("ps_ao", [P, CT], F32))
        ps_misc = ctx.enter_context(nc.psum_tensor("ps_misc", [P, BANKS, CT], F32))

        def w(name, j=0):
            at = WCOLS[name][0] - W_FIRST + j * D
            return W[:, at:at + D]

        first = hT[:, :, :].rearrange("p j t -> p (j t)")[:, 0:W_FIRST]

        def w_first(name, j):
            return first[:, WCOLS[name][0] + j * D:WCOLS[name][0] + (j + 1) * D]

        def bcol(name):
            return bias[:, BIAS[name]:BIAS[name] + 1]

        def const(name):
            at, n = CONST[name]
            return cst[:, at:at + n]

        ident = const("ident")
        condT = first[:, WCOLS["condT"][0]:WCOLS["condT"][0] + B]

        names = ["rows_in", "x_in0", "x_in1", "x_in2", "x_in3", "ctxT_in", "ctx_in", "small_in", "weights_in",
                 "rest_in", "stored", "dve_chain", "fixed_ready", "sums_zeroed", "exp_done", "silu_done",
                 "mod_products", "vec_ready", "var_ready", "vareps_ready", "rstd_ready", "xn_ready", "cn_ready",
                 "xnT_ready", "cnT_ready", "misc_filled", "rope_read", "rope_sums", "q_high", "q_low", "k_high",
                 "k_low", "v_ready", "kd_in0", "kd_in1", "kd_in2", "kd_in3", "zeros_ready", "max_scores",
                 "max_taken", "maxT_ready", "q_stored0", "q_stored1", "k_stored0", "k_stored1", "max_stored",
                 "keys_in0", "keys_in1", "queries_in0", "queries_in1", "queries_in2", "maxima_in0",
                 "maxima_in1", "maxima_in2", "scores_ready", "probs_ready", "values_done", "sums_copied",
                 "x_biased", "rden_ready", "att_ready", "attT_ready", "hT_ready", "y_ready", "x_ready"]
        S = {n: sem(n) for n in names}
        GROUPS = NG * CB

        def bank(n):
            return ps_misc[:, n % BANKS, :]

        sources = {(st.kind, st.f): st.use for st in plan if st.kind in ("k", "q")}
        for st in plan:
            if st.kind in ("khi", "klo", "qhi", "qlo"):
                st.source = sources[st.kind[0], st.f]
        norm_use = [st.use for st in plan if st.kind == "norm"]
        biased = 0
        for st in plan:
            biased += st.kind == "bias"
            st.biased = biased
        mT_use = [st.use for st in plan if st.kind == "mT"]

        def f32(tile):
            return tile.bitcast(F32)

        def ns_of(st):
            return NS_CTX if ATTN[st.a]["cross"] else P

        feeds = {}
        update = {s: 0 for s in range(STREAMS)}
        normed = {s: 0 for s in range(STREAMS)}
        norms = [st for st in plan if st.kind in ("stats", "cstats")]
        for number, st in enumerate(norms):
            st.norm_no = number
        numbers = {(st.kind[-5:] == "stats" and st.kind[0] == "c", st.f, st.m): st.norm_no for st in norms}
        for st in plan:
            if st.kind in ("ln", "cln"):
                st.norm_no = numbers[st.kind == "cln", st.f, st.m]
        for st in plan:
            if st.kind == "ln" and st.m is None:
                feeds[st.f] = st.k
            if st.kind == "ln" and st.m is not None:
                feeds["mlp", st.m] = st.k
            if st.kind in ("stats", "store"):
                st.after = update[st.s]
            if st.kind in ("yT", "out"):
                update[st.s] = st.update
                st.norms_before = normed[st.s]
            if st.kind == "bias":
                st.norms_before = normed[st.s]
            if st.kind == "ln":
                normed[st.s] = st.k + 1

        xT_use = {st.k: st.use for st in plan if st.kind == "xT"}
        v_after_cT = {st.s: st.f + 1 for st in plan if st.kind == "v" and st.a == 1}

        def key_source(st):
            if not ATTN[st.a]["cross"]:
                return xnT[:, feeds[st.f] % 2, :]
            return cnT[:, :] if st.a == 1 else crawT[:, st.s, :]

        with nc.Block() as block:
            @block.sync
            def _(sp):
                def load_x(s):
                    sp.dma_start(x[:, s, :, :].rearrange("p b f -> p (b f)"),
                                 x_in[:, s * CB * D:(s + 1) * CB * D]).then_inc(S[f"x_in{s}"], 16)

                load_x(0)
                sp.dma_start(first, weights[:, 0:W_FIRST]).then_inc(S["small_in"], 16)
                sp.dma_start(W[:, 0:W_SECOND - W_FIRST], weights[:, W_FIRST:W_SECOND]).then_inc(S["weights_in"], 16)
                for s in range(1, STREAMS):
                    load_x(s)
                sp.dma_start(craw[0:NS_CTX, :, :, :].rearrange("p s b f -> p (s b f)"),
                             ctx_in).then_inc(S["ctx_in"], 16)
                sp.dma_start(crawT[:, :, :].rearrange("p s t -> p (s t)"), ctxT_in).then_inc(S["ctxT_in"], 16)
                sp.dma_start(W[:, W_SECOND - W_FIRST:W_TOTAL - W_FIRST],
                             weights[:, W_SECOND:W_TOTAL]).then_inc(S["rest_in"], 16)
                sp.dma_start(bias_rows[:, :, :].rearrange("p a f -> p (a f)"), rows_in).then_inc(S["rows_in"], 16)
                for st in plan:
                    if st.kind == "kstore":
                        sp.wait_ge(S["k_high"], st.f + 1)
                        sp.dma_start(k_mem[st.f, :, 0:3:2, :], f32(Kh[:, st.f % 2, :])[:, None, :].to_broadcast(
                            [P, 2, CT])).then_inc(S[f"k_stored{st.f % 2}"], 16)
                        sp.wait_ge(S["k_low"], st.f + 1)
                        sp.dma_start(k_mem[st.f, :, 1, :], f32(Kl[:, :])).then_inc(S[f"k_stored{st.f % 2}"], 16)
                    elif st.kind == "qstore":
                        sp.wait_ge(S["q_high"], st.f + 1)
                        sp.dma_start(q_mem[st.f, :, 0:2, :], f32(Qh[:, st.f % 2, :])[:, None, :].to_broadcast(
                            [P, 2, CT])).then_inc(S[f"q_stored{st.f % 2}"], 16)
                        sp.wait_ge(S["q_low"], st.f + 1)
                        sp.dma_start(q_mem[st.f, :, 2, :], f32(Ql[:, :])).then_inc(S[f"q_stored{st.f % 2}"], 16)
                    elif st.kind == "kmask":
                        n, r = CB * ns_of(st), slice(HD * st.h, HD * st.h + HD)
                        if st.h == 0:
                            sp.wait_ge(S["k_high"], st.f + 1)
                        if st.h % HG == 0:
                            if st.f:
                                sp.wait_ge(S["max_scores"], CB * (NG * (st.f - 1) + st.h // HG + 1))
                            elif st.h == 0:
                                sp.wait_ge(S["zeros_ready"], 2)
                        sp.dma_start(f32(Kd[r, st.h, 0:n]),
                                     f32(Kh[r, st.f % 2, 0:n])).then_inc(S[f"kd_in{st.h // HG}"], 16)
                    elif st.kind == "kload":
                        n = CB * ns_of(st)
                        sp.wait_ge(S[f"k_stored{st.f % 2}"], 32 * (st.f // 2 + 1))
                        if st.f >= 2:
                            sp.wait_ge(S["scores_ready"], GROUPS * (st.f - 1))
                        sp.dma_start(f32(Ks[0:SROWS, st.f % 2, :, 0:n]),
                                     k_mem[st.f].rearrange("(n r) s t -> (r s) n t", n=NG)[:, :, 0:n]
                                     ).then_inc(S[f"keys_in{st.f % 2}"], 16)
                    elif st.kind == "qload":
                        half = 2 * st.f + st.g
                        sp.wait_ge(S[f"q_stored{st.f % 2}"], 32 * (st.f // 2 + 1))
                        if half >= 3:
                            sp.wait_ge(S["scores_ready"], GROUPS // 2 * (half - 2))
                        else:
                            sp.wait_ge(S["fixed_ready"], (3, 5, 6)[half])
                        heads = q_mem[st.f].rearrange("(n c r) s t -> c (r s) n t", n=NG, c=HG)
                        for c in range(HG):
                            sp.dma_start(f32(Qd[SR * c:SR * c + SR, half % 3, :, c, :]),
                                         heads[c][:, GP * st.g:GP * st.g + GP, :]
                                         ).then_inc(S[f"queries_in{half % 3}"], 16)
                    elif st.kind == "mstore":
                        sp.wait_ge(S["maxT_ready"], st.f + 1)
                        sp.dma_start(m_mem[st.f], f32(maxT[:, :])).then_inc(S["max_stored"], 16)
                    elif st.kind == "mload":
                        half = 2 * st.f + st.g
                        sp.wait_ge(S["max_stored"], 16 * (st.f + 1))
                        if half >= 3:
                            sp.wait_ge(S["scores_ready"], GROUPS // 2 * (half - 2))
                        sp.dma_start(f32(Qd[SROWS:SROWS + 1, half % 3, :, :, :]).rearrange("a n c t -> a (n c t)"),
                                     m_mem[st.f, GH * st.g:GH * st.g + GH, :].rearrange("(a h) t -> a (h t)", a=1)
                                     ).then_inc(S[f"maxima_in{half % 3}"], 16)
                    elif st.kind == "store":
                        sp.wait_ge(S["x_ready"], st.after)
                        sp.dma_start(out[:, st.s * CB * D:(st.s + 1) * CB * D],
                                     x[:, st.s, :, :].rearrange("p b f -> p (b f)")).then_inc(S["stored"], 16)
                sp.wait_ge(S["stored"], 16 * STREAMS)

            @block.vector
            def _(dve):
                chain = [0]

                def link(ins):
                    chain[0] += 1
                    return ins.then_inc(S["dve_chain"], 1)

                def linked():
                    dve.wait_ge(S["dve_chain"], chain[0])

                def statistics(src, rows, which):
                    for b in range(CB):
                        link(dve.bn_stats(stats[0:rows, which, b, :], src[0:rows, b, :]))
                    linked()
                    for b in range(CB):
                        dve.bn_aggr(mv[0:rows, which, b, :],
                                    stats[0:rows, which, b, :]).then_inc(S["var_ready"], 1)

                def norm(src, rows, dst, which, rstd_no, ready):
                    dve.wait_ge(S["rstd_ready"], rstd_no)
                    for b in range(CB):
                        dve.tensor_scalar(dst[0:rows, b, :], src[0:rows, b, :], mv[0:rows, which, b, 0:1],
                                          rstd[0:rows, which, b:b + 1], ALU.subtract,
                                          ALU.mult).then_inc(ready, 1)

                def rope(st):
                    ns, sums = (ns_of(st), 2 * rope_no(st.f)) if st.kind == "k" else (P, 2 * rope_no(st.f) + 1)
                    n = CB * ns
                    dve.wait_ge(S["k_low" if st.kind == "k" else "q_low"], st.f)
                    if sums:
                        dve.wait_ge(S["rope_sums"], sums)
                    total = ropeA[:, sums % 2, :]
                    for i, dst, table in ((0, total, "cos"), (1, ropeB, "sin")):
                        dve.wait_ge(S["misc_filled"], st.use + i + 1)
                        dve.tensor_tensor(dst[:, 0:n].rearrange("p (b t) -> p b t", b=CB),
                                          bank(st.use + i)[:, 0:n].rearrange("p (b t) -> p b t", b=CB),
                                          const(table)[:, None, 0:ns].to_broadcast([P, CB, ns]),
                                          ALU.mult).then_inc(S["rope_read"], 1)
                    dve.wait_ge(S["rope_read"], 2 * (sums + 1))
                    dve.tensor_tensor(total[:, 0:n], total[:, 0:n], ropeB[:, 0:n],
                                      ALU.add).then_inc(S["rope_sums"], 1)

                def low(st, high, dst, ready, stored, name, n):
                    if st.f:
                        dve.wait_ge(S[f"{stored}{(st.f - 1) % 2}"], 32 * ((st.f - 1) // 2 + 1))
                    if ATTN[st.a]["rope"]:
                        ins = dve.tensor_tensor(dst[:, 0:n], ropeA[:, int(st.kind[0] == "q"), 0:n],
                                                high[:, 0:n], ALU.subtract)
                    else:
                        ins = dve.scalar_tensor_tensor(dst[:, 0:n], bank(st.source)[:, 0:n], bcol(name),
                                                       high[:, 0:n], ALU.add, ALU.subtract)
                    ins.then_inc(S[ready], 1)

                def condition():
                    dve.wait_ge(S["exp_done"], 1)
                    link(dve.tensor_scalar(silu[:, 1, :], silu[:, 0, :], 1.0, None, ALU.add))
                    linked()
                    link(dve.reciprocal(silu[:, 0, :], silu[:, 1, :]))
                    linked()
                    dve.tensor_tensor(silu[:, 2, :], condT, silu[:, 0, :], ALU.mult).then_inc(S["silu_done"], 1)

                def modulation():
                    dve.wait_ge(S["mod_products"], 1)
                    for v in range(NV):
                        name = f"mod{v}" if v < 6 else f"ln{v - 6}"
                        one = 1.0 if v in (MULT_A, MULT_M, MULT_1, MULT_2, MULT_3) else 0.0
                        dve.tensor_scalar(vec[:, :, v], ps_sc[:, 0, v * B:(v + 1) * B], bcol(name), one,
                                          ALU.add, ALU.add).then_inc(S["vec_ready"], 1)

                dve.memset(ps_ao[:, :], 0.0).then_inc(S["sums_zeroed"], 1)
                for st in late:
                    if st.kind == "stats":
                        if st.after:
                            dve.wait_ge(S["x_ready"], st.after)
                        else:
                            dve.wait_ge(S[f"x_in{st.s}"], 16)
                        statistics(x[:, st.s, :, :], P, 0)
                        if st.k == 0:
                            condition()
                    elif st.kind == "cstats":
                        dve.wait_ge(S["ctx_in"], 16)
                        statistics(craw[:, st.s, :, :], NS_CTX, 1)
                    elif st.kind == "ln":
                        if st.k:
                            dve.wait_ge(S["misc_filled"], xT_use[st.k - 1] + 1)
                        norm(x[:, st.s, :, :], P, xn, 0, st.norm_no + 1, S["xn_ready"])
                        if st.k == 0:
                            for g in range(2):
                                dve.memset(f32(Kd[:, g * GH:(g + 1) * GH, :]), 0.0).then_inc(S["zeros_ready"], 1)
                                if g == 0:
                                    modulation()
                    elif st.kind == "cln":
                        if st.k:
                            dve.wait_ge(S["cnT_ready"], st.k)
                        norm(craw[:, st.s, :, :], NS_CTX, cn, 1, st.norm_no + 1, S["cn_ready"])
                    elif st.kind in ("k", "q") and ATTN[st.a]["rope"]:
                        rope(st)
                    elif st.kind == "klo":
                        dve.wait_ge(S["k_high"], st.f + 1)
                        low(st, Kh[:, st.f % 2, :], Kl, "k_low", "k_stored", f"k{st.a}", CB * ns_of(st))
                    elif st.kind == "qlo":
                        dve.wait_ge(S["q_high"], st.f + 1)
                        low(st, Qh[:, st.f % 2, :], Ql, "q_low", "q_stored", f"q{st.a}", CT)
                    elif st.kind == "max":
                        ns = ns_of(st)
                        dve.wait_ge(S["max_scores"], st.k + 1)
                        dst = maxima[:, st.b, HG * st.n:HG * st.n + HG]
                        if st.n == 0 and st.b == 0 and st.f:
                            dve.wait_ge(S["misc_filled"], mT_use[st.f - 1] + 1)
                        dve.tensor_reduce(dst, ps_max[:, st.k % MAX_BANKS, 0:HG * ns].rearrange(
                            "p (h k) -> p h k", h=HG), AX_X, ALU.max, negate=True).then_inc(S["max_taken"], 1)
                    elif st.kind == "norm":
                        turned = bank(st.use).rearrange("p (b n c r) -> p b (n c) r", b=2, n=GP, c=HG)
                        dve.wait_ge(S["misc_filled"], st.use + 1)
                        dve.reciprocal(rden[:, st.k % 2, :, :], turned[:, :, :, HD]).then_inc(S["rden_ready"], 1)
                        dve.wait_ge(S["rden_ready"], st.k + 1)
                        if st.b == 0 and st.g == 0 and st.f:
                            dve.wait_ge(S["attT_ready"], st.f)
                        for i in range(2):
                            dve.tensor_tensor(att[:, st.b + i, GH * HD * st.g:GH * HD * (st.g + 1)].rearrange(
                                "p (h d) -> p h d", h=GH), turned[:, i, :, 0:HD],
                                rden[:, st.k % 2, i, :][:, :, None].to_broadcast([P, GH, HD]),
                                ALU.mult).then_inc(S["att_ready"], 1)
                    elif st.kind in ("o", "h2"):
                        if st.kind == "o":
                            gate = ATTN[st.a]["gate"]
                            add = bcol(f"o{st.a}") if ATTN[st.a]["bias"] else None
                        else:
                            gate, add = MLP[st.a]["gate"], bcol(f"b2_{st.a}")
                        dve.wait_ge(S["misc_filled"], st.use + 1)
                        src = bank(st.use)
                        if gate is not None:
                            for b in range(CB):
                                c = st.s * CB + b
                                ins = dve.tensor_scalar(yT_sb[:, b * P:(b + 1) * P], src[:, b * P:(b + 1) * P],
                                                        add, vec[:, c, gate:gate + 1], ALU.add, ALU.mult)
                        elif add is not None:
                            ins = dve.tensor_scalar(yT_sb[:, :], src, add, None, ALU.add)
                        else:
                            ins = dve.tensor_copy(yT_sb[:, :], src)
                        ins.then_inc(S["y_ready"], 1)
                    elif st.kind in ("yT", "out"):
                        dve.wait_ge(S["misc_filled"], st.use + 1)
                        dve.wait_ge(S["xn_ready"], CB * st.norms_before)
                        if st.biased:
                            dve.wait_ge(S["x_biased"], st.biased)
                        flat = x[:, st.s, :, :].rearrange("p b f -> p (b f)")
                        dve.tensor_tensor(flat, bank(st.use), flat, ALU.add).then_inc(S["x_ready"], 1)

            @block.gpsimd
            def _(pool):
                def fill(number, tile, value):
                    if number:
                        pool.wait_ge(S["fixed_ready"], number)
                    pool.memset(tile, value).then_inc(S["fixed_ready"], 1)

                fill(0, minus_half[:, :], -0.5)
                fill(1, V[:, :, :, :, :], 1.0)
                for st in plan:
                    if st.kind in ("stats", "cstats"):
                        rows, which, eps = (P, 0, st.spec["eps"]) if st.kind == "stats" else (NS_CTX, 1, 1e-6)
                        pool.wait_ge(S["var_ready"], CB * (st.norm_no + 1))
                        pool.tensor_scalar(vareps[0:rows, which, :], mv[0:rows, which, :, 1], eps, None,
                                           ALU.add).then_inc(S["vareps_ready"], 1)
                        pool.wait_ge(S["vareps_ready"], st.norm_no + 1)
                        pool.tensor_tensor(rstd[0:rows, which, :], vareps[0:rows, which, :],
                                           minus_half[0:rows, :], ALU.pow).then_inc(S["rstd_ready"], 1)
                        if st.norm_no == 0:
                            fill(2, f32(Qd[0:SROWS, 0, :, :, :]), 0.0)
                            fill(3, f32(Ks[SROWS:SROWS + 1, :, :, :]), 1.0)
                            fill(4, f32(Qd[0:SROWS, 1, :, :, :]), 0.0)
                            fill(5, f32(Qd[0:SROWS, 2, :, :, :]), 0.0)
                    elif st.kind == "bias":
                        pool.wait_ge(S["xn_ready"], CB * st.norms_before)
                        which = 0 if st.m is None else 1
                        if st.k == 0:
                            pool.wait_ge(S["rows_in"], 16)
                        pool.tensor_tensor(x[:, st.s, :, :], x[:, st.s, :, :],
                                           bias_rows[:, which, :][:, None, :].to_broadcast([P, CB, D]),
                                           ALU.add).then_inc(S["x_biased"], 1)

            @block.scalar
            def _(act):
                act.dma_start(bias[:, :], biases).then_inc(S["small_in"], 16)
                act.dma_start(cst[:, :], consts).then_inc(S["small_in"], 16)
                act.wait_ge(S["small_in"], 48)
                act.activation(silu[:, 0, :], condT, ACT.Exp, scale=-1.0).then_inc(S["exp_done"], 1)
                for st in late:
                    if st.kind == "cT":
                        act.wait_ge(S["misc_filled"], st.use + 1)
                        if st.k:
                            act.wait_ge(S["v_ready"], v_after_cT[st.k - 1])
                        act.activation(cnT[:, :], bank(st.use)[:, 0:CB * NS_CTX],
                                       ACT.Copy).then_inc(S["cnT_ready"], 1)
                    elif st.kind in ("khi", "qhi"):
                        k = st.kind == "khi"
                        n = CB * ns_of(st) if k else CT
                        high = (Kh if k else Qh)[:, st.f % 2, 0:n]
                        if st.f >= 2:
                            if k:
                                act.wait_ge(S[f"k_stored{st.f % 2}"], 32 * (st.f // 2))
                                act.wait_ge(S["max_scores"], GROUPS * (st.f - 1))
                            else:
                                act.wait_ge(S[f"q_stored{st.f % 2}"], 32 * (st.f // 2))
                                act.wait_ge(S["max_scores"], GROUPS * (st.f - 1))
                        if ATTN[st.a]["rope"]:
                            act.wait_ge(S["rope_sums"], 2 * rope_no(st.f) + (1 if k else 2))
                            ins = act.activation(high, ropeA[:, int(not k), 0:n], ACT.Copy)
                        else:
                            act.wait_ge(S["misc_filled"], st.source + 1)
                            ins = act.activation(high, bank(st.source)[:, 0:n], ACT.Identity,
                                                 bias=bcol(f"k{st.a}" if k else f"q{st.a}"))
                        ins.then_inc(S["k_high" if k else "q_high"], 1)
                    elif st.kind == "v":
                        ns = ns_of(st)
                        act.wait_ge(S["misc_filled"], st.use + 1)
                        if st.f >= 3:
                            act.wait_ge(S["values_done"], GROUPS * (st.f - 2))
                        elif st.f == 0:
                            act.wait_ge(S["fixed_ready"], 2)
                        act.activation(V[0:ns, st.f % 3, :, :, 0:HD],
                                       bank(st.use)[0:ns, :].rearrange("p (b h d) -> p b h d", b=CB, h=H),
                                       ACT.Copy).then_inc(S["v_ready"], 1)
                    elif st.kind == "xT":
                        act.wait_ge(S["misc_filled"], st.use + 1)
                        if st.k == 0:
                            act.wait_ge(S["vec_ready"], NV)
                        src, dst = bank(st.use), xnT[:, st.k % 2, :]
                        if st.spec["mult"] is None:
                            act.activation(dst, src, ACT.Copy).then_inc(S["xnT_ready"], CB)
                        else:
                            for b in range(CB):
                                c, m, sh = st.s * CB + b, st.spec["mult"], st.spec["shift"]
                                act.activation(dst[:, b * P:(b + 1) * P], src[:, b * P:(b + 1) * P], ACT.Identity,
                                               scale=vec[:, c, m:m + 1],
                                               bias=vec[:, c, sh:sh + 1]).then_inc(S["xnT_ready"], 1)
                    elif st.kind == "mT":
                        act.wait_ge(S["misc_filled"], st.use + 1)
                        if st.f:
                            act.wait_ge(S["max_stored"], 16 * st.f)
                        act.activation(maxT[:, :], bank(st.use)[0:H, :], ACT.Copy).then_inc(S["maxT_ready"], 1)
                    elif st.kind == "score":
                        ns = ns_of(st)
                        act.wait_ge(S["scores_ready"], st.k + 1)
                        if st.k >= 4:
                            act.wait_ge(S["values_done"], st.k - 3)
                        act.activation(PT[0:ns, st.k % 4, :], ps_sc[0:ns, st.k % 2, :], ACT.Exp,
                                       scale=SCALE).then_inc(S["probs_ready"], 1)
                    elif st.kind == "copy":
                        act.wait_ge(S["values_done"], HG * (st.k + 1))
                        if st.k >= 2:
                            act.wait_ge(S["misc_filled"], norm_use[st.k - 2] + 1)
                        act.activation(AOs[:, st.k % 2, :], ps_ao[:, :], ACT.Copy).then_inc(S["sums_copied"], 1)
                    elif st.kind == "aT":
                        act.wait_ge(S["misc_filled"], st.use + 1)
                        if ATTN[st.a]["bias"]:
                            ins = act.activation(attT[:, :], bank(st.use), ACT.Identity, bias=bcol(f"v{st.a}"))
                        else:
                            ins = act.activation(attT[:, :], bank(st.use), ACT.Copy)
                        ins.then_inc(S["attT_ready"], 1)
                    elif st.kind == "h":
                        act.wait_ge(S["misc_filled"], st.use + 1)
                        act.activation(hT[:, st.j, :], bank(st.use),
                                       ACT.Gelu_apprx_tanh if MLP[st.a]["act"] == "tanh" else ACT.Gelu,
                                       bias=bcol(f"b1_{st.a}_{st.j}")).then_inc(S["hT_ready"], 1)

            @block.tensor
            def _(pe):
                def fill(n):
                    if n >= BANKS:
                        pe.wait_ge(S[uses[n - BANKS][0]], uses[n - BANKS][1])

                def turn(src, use, rows=P):
                    for b in range(CB):
                        last = pe.transpose(bank(use)[:, b * rows:(b + 1) * rows], src[0:rows, b, :],
                                            ident[0:rows, 0:rows])
                    last.then_inc(S["misc_filled"], 1)

                pe.wait_ge(S["silu_done"], 1)
                for v in range(NV):
                    lhs, rhs = ((w_first("mod", v), silu[:, 2, :]) if v < 6 else
                                (w_first("ln", v - 6), condT))
                    last = pe.matmul(ps_sc[:, 0, v * B:(v + 1) * B], lhs, rhs, start=True, stop=True)
                last.then_inc(S["mod_products"], 1)
                for st in plan:
                    if st.kind == "xT":
                        fill(st.use)
                        pe.wait_ge(S["xn_ready"], CB * (st.k + 1))
                        turn(xn, st.use)
                    elif st.kind == "cT":
                        fill(st.use)
                        pe.wait_ge(S["cn_ready"], CB * (st.k + 1))
                        turn(cn, st.use, NS_CTX)
                    elif st.kind in ("k", "q"):
                        n = CB * (ns_of(st) if st.kind == "k" else P)
                        if st.kind == "k":
                            if st.a == 0 or st.a == 2:
                                pe.wait_ge(S["xnT_ready"], CB * (feeds[st.f] + 1))
                            elif st.a == 1:
                                pe.wait_ge(S["cnT_ready"], st.s + 1)
                            else:
                                pe.wait_ge(S["ctxT_in"], 16)
                            if st.f == 0:
                                pe.wait_ge(S["weights_in"], 16)
                            src = key_source(st)
                        else:
                            pe.wait_ge(S["xnT_ready"], CB * (feeds[st.f] + 1))
                            src = xnT[:, feeds[st.f] % 2, :]
                        forms = ["", "s"] if ATTN[st.a]["rope"] else [""]
                        for i, form in enumerate(forms):
                            fill(st.use + i)
                            pe.matmul(bank(st.use + i)[:, 0:n], w(f"{st.kind}{st.a}{form}"), src[:, 0:n],
                                      start=True, stop=True).then_inc(S["misc_filled"], 1)
                    elif st.kind == "v":
                        ns = ns_of(st)
                        fill(st.use)
                        src = key_source(st)
                        for b in range(CB):
                            last = pe.matmul(bank(st.use)[0:ns, b * D:(b + 1) * D], src[:, b * ns:(b + 1) * ns],
                                             w(f"v{st.a}"), start=True, stop=True)
                        last.then_inc(S["misc_filled"], 1)
                    elif st.kind == "max":
                        ns = ns_of(st)
                        if st.b == 0:
                            pe.wait_ge(S[f"kd_in{st.n}"], 16 * HG * (st.f + 1))
                        if st.b == 0 and st.n == 0:
                            pe.wait_ge(S["q_high"], st.f + 1)
                        if st.k >= MAX_BANKS:
                            pe.wait_ge(S["max_taken"], st.k - MAX_BANKS + 1)
                        pe.matmul(ps_max[:, st.k % MAX_BANKS, 0:HG * ns], Qh[:, st.f % 2, st.b * P:(st.b + 1) * P],
                                  Kd[:, HG * st.n:HG * st.n + HG, st.b * ns:(st.b + 1) * ns],
                                  start=True, stop=True).then_inc(S["max_scores"], 1)
                    elif st.kind == "mT":
                        fill(st.use)
                        pe.wait_ge(S["max_taken"], GROUPS * (st.f + 1))
                        for b in range(CB):
                            last = pe.transpose(bank(st.use)[0:H, b * P:(b + 1) * P], maxima[:, b, :], ident)
                        last.then_inc(S["misc_filled"], 1)
                    elif st.kind == "score":
                        ns, half = ns_of(st), 2 * st.f + st.n // GP
                        if st.b == 0 and st.n % GP == 0:
                            pe.wait_ge(S[f"queries_in{half % 3}"], 16 * HG * (half // 3 + 1))
                            pe.wait_ge(S[f"maxima_in{half % 3}"], 16 * (half // 3 + 1))
                        if st.b == 0 and st.n == 0:
                            pe.wait_ge(S[f"keys_in{st.f % 2}"], 16 * (st.f // 2 + 1))
                            if st.f == 0:
                                pe.wait_ge(S["fixed_ready"], 4)
                        if st.k >= 2:
                            pe.wait_ge(S["probs_ready"], st.k - 1)
                        pe.matmul(ps_sc[0:ns, st.k % 2, :], Ks[:, st.f % 2, st.n, st.b * ns:(st.b + 1) * ns],
                                  Qd[:, half % 3, st.n % GP, :, st.b * P:(st.b + 1) * P],
                                  start=True, stop=True).then_inc(S["scores_ready"], 1)
                    elif st.kind == "value":
                        ns = ns_of(st)
                        pe.wait_ge(S["probs_ready"], st.k + 1)
                        if st.b == 0 and st.n == 0:
                            pe.wait_ge(S["v_ready"], st.f + 1)
                        if st.k % NG == 0 and st.k:
                            pe.wait_ge(S["sums_copied"], st.k // NG)
                        at = (st.b % 2 * GP + st.n % GP) * P
                        for c in range(HG):
                            last = pe.matmul(ps_ao[32 * c:32 * c + VW, at:at + P],
                                             V[0:ns, st.f % 3, st.b, HG * st.n + c, :],
                                             PT[0:ns, st.k % 4, c * P:(c + 1) * P], start=True, stop=True)
                        last.then_inc(S["values_done"], 1)
                    elif st.kind == "norm":
                        fill(st.use)
                        pe.wait_ge(S["sums_copied"], st.k + 1)
                        for n in range(NG):
                            last = pe.transpose(bank(st.use)[:, n * P:(n + 1) * P],
                                                AOs[:, st.k % 2, n * P:(n + 1) * P], ident)
                        last.then_inc(S["misc_filled"], 1)
                    elif st.kind == "aT":
                        fill(st.use)
                        pe.wait_ge(S["att_ready"], 2 * CB * (st.f + 1))
                        turn(att, st.use)
                    elif st.kind == "o":
                        fill(st.use)
                        pe.wait_ge(S["attT_ready"], st.f + 1)
                        pe.matmul(bank(st.use), w(f"o{st.a}"), attT[:, :], start=True,
                                  stop=True).then_inc(S["misc_filled"], 1)
                    elif st.kind == "h":
                        fill(st.use)
                        pe.wait_ge(S["xnT_ready"], CB * (feeds["mlp", st.m] + 1))
                        if st.k == 0:
                            pe.wait_ge(S["rest_in"], 16)
                        pe.matmul(bank(st.use), w(f"w1_{st.a}", st.j), xnT[:, feeds["mlp", st.m] % 2, :],
                                  start=True, stop=True).then_inc(S["misc_filled"], 1)
                    elif st.kind == "h2":
                        fill(st.use)
                        pe.wait_ge(S["hT_ready"], FF * (st.m + 1))
                        for j in range(FF):
                            last = pe.matmul(bank(st.use), w(f"w2_{st.a}", j), hT[:, j, :], start=(j == 0),
                                             stop=(j == FF - 1))
                        last.then_inc(S["misc_filled"], 1)
                    elif st.kind == "out":
                        fill(st.use)
                        if st.m is None:
                            pe.wait_ge(S["attT_ready"], st.f + 1)
                            parts = [(attT[:, :], w(f"o{st.a}"))]
                        else:
                            pe.wait_ge(S["hT_ready"], FF * (st.m + 1))
                            parts = [(hT[:, j, :], w(f"w2_{st.a}", j)) for j in range(FF)]
                        for b in range(CB):
                            for i, (src, weight) in enumerate(parts):
                                last = pe.matmul(bank(st.use)[:, b * D:(b + 1) * D], src[:, b * P:(b + 1) * P],
                                                 weight, start=(i == 0), stop=(i == len(parts) - 1))
                        last.then_inc(S["misc_filled"], 1)
                    elif st.kind == "yT":
                        fill(st.use)
                        pe.wait_ge(S["y_ready"], st.k + 1)
                        for b in range(CB):
                            last = pe.transpose(bank(st.use)[:, b * P:(b + 1) * P], yT_sb[:, b * P:(b + 1) * P],
                                                ident)
                        last.then_inc(S["misc_filled"], 1)


def _constants():
    c = np.zeros((P, NCONST), np.float32)
    p = np.arange(P)
    at = CONST["ident"][0]
    c[p, at + p] = 1.0
    half = HD // 2
    inv = (1.0 / np.float32(10000.0) ** (np.arange(half, dtype=np.float32) / half)).astype(np.float32)
    ang = (np.arange(P, dtype=np.float32)[None, :] * inv[p % half][:, None]).astype(np.float32)
    at = CONST["cos"][0]
    c[:, at:at + P] = np.cos(ang)
    at = CONST["sin"][0]
    c[:, at:at + P] = np.sin(ang) * np.where(p % HD < half, -1.0, 1.0)[:, None].astype(np.float32)
    return c


def kernel(**inputs):
    import concourse.bacc as _bacc
    from concourse.bass_utils import run_bass_kernel_spmd as _run

    i = {n: np.asarray(a) for n, a in inputs.items()}
    L0, L1 = "L0_xcond_", "L1_xcond_"

    def blocks(a):
        return a.reshape(-1, P, a.shape[1]).transpose(1, 0, 2).reshape(P, -1)

    swap = (np.arange(D) // HD) * HD + (np.arange(D) + HD // 2) % HD
    qkv0, kvc0 = i[L0 + "W_qkv"], i[L0 + "W_kvc"]
    qkv1 = i[L1 + "qkv_w"].T
    parts = {
        "mod": i[L0 + "W_mod"],
        "ln": np.concatenate([i[L1 + f"ln{n}_w"].T for n in (1, 2, 3)], axis=1),
        "condT": i["cond_1024"].T,
        "q0": qkv0[:, 0:D], "k0": qkv0[:, D:2 * D], "v0": qkv0[:, 2 * D:], "o0": i[L0 + "W_proj"],
        "q1": i[L0 + "W_qc"], "k1": kvc0[:, 0:D], "v1": kvc0[:, D:], "o1": i[L0 + "W_cproj"],
        "w1_0": i[L0 + "W_mlp1"], "w2_0": blocks(i[L0 + "W_mlp2"]),
        "q2": qkv1[:, 0:D], "q2s": qkv1[:, 0:D][:, swap], "k2": qkv1[:, D:2 * D],
        "k2s": qkv1[:, D:2 * D][:, swap], "v2": qkv1[:, 2 * D:], "o2": i[L1 + "sa_out_w"].T,
        "q3": i[L1 + "q_w"].T, "q3s": i[L1 + "q_w"].T[:, swap], "k3": i[L1 + "k_w"].T,
        "k3s": i[L1 + "k_w"].T[:, swap], "v3": i[L1 + "v_w"].T, "o3": i[L1 + "ca_out_w"].T,
        "w1_1": i[L1 + "ffn_w1"].T, "w2_1": blocks(i[L1 + "ffn_w2"].T),
    }
    weights = np.concatenate([parts[n] for n in WCOLS], axis=1)
    bq = i[L0 + "b_qkv"].reshape(3, D)
    bkv = i[L0 + "b_kvc"].reshape(2, D)
    biases = np.concatenate([
        i[L0 + "b_mod"].reshape(6, D), i[L1 + "ln1_b"].reshape(2, D), i[L1 + "ln2_b"].reshape(2, D),
        i[L1 + "ln3_b"].reshape(2, D), bq, i[L0 + "b_proj"][None], i[L0 + "b_qc"][None], bkv,
        i[L0 + "b_cproj"][None], i[L0 + "b_mlp1"].reshape(FF, D), i[L0 + "b_mlp2"][None],
        i[L1 + "ffn_b1"].reshape(FF, D), i[L1 + "ffn_b2"][None]], axis=0).T
    arrays = {
        "weights": weights, "biases": biases, "consts": _constants(),
        "x_in": i["x"].transpose(1, 0, 2).reshape(P, B * D),
        "ctx_in": i["ctx_1024"].transpose(1, 0, 2).reshape(NS_CTX, B * D),
        "ctxT_in": i["ctx_1024"].transpose(2, 0, 1).reshape(D, B * NS_CTX),
        "rows_in": np.broadcast_to(np.concatenate([i[L0 + "b_cproj"], i[L1 + "ffn_b2"]]), (P, 2 * D)),
    }
    arrays = {n: np.ascontiguousarray(a) for n, a in arrays.items()}
    nc = _bacc.Bacc("TRN2", target_bir_lowering=False, num_devices=1)
    args = [nc.dram_tensor(n, a.shape, F32, kind="ExternalInput").ap() for n, a in arrays.items()]
    out = nc.dram_tensor("out", (P, B * D), F32, kind="ExternalOutput").ap()
    units = len(ATTN) * STREAMS
    mem = [nc.dram_tensor(n, shape, F32, kind="Internal").ap() for n, shape in
           (("q_mem", (units, P, SPLIT, CT)), ("k_mem", (units, P, SPLIT, CT)), ("m_mem", (units, H, CT)))]
    block_kernel(nc, *args, *mem, out)
    r = _run(nc, [arrays], core_ids=[0])
    return np.ascontiguousarray(np.asarray(r.results[0]["out"]).reshape(P, B, D).transpose(1, 0, 2))
```
